# Optimizing a Trainium2 kernel written in Bass

```python
import numpy as np
import jax
import jax.numpy as jnp

def _softmax(x, axis=-1):
    return jax.nn.softmax(x, axis=axis)

def _gelu(x):
    return jax.nn.gelu(x, approximate=True)

def _silu(x):
    return jax.nn.silu(x)

def _sigmoid(x):
    return jax.nn.sigmoid(x)

def _layernorm(x, axis=-1, eps=1e-05):
    m = jnp.mean(x, axis=axis, keepdims=True)
    v = jnp.var(x, axis=axis, keepdims=True)
    return (x - m) / jnp.sqrt(v + eps)

def _scatter_add(tgt, idx, src, axis=0):
    return tgt.at[idx].add(src)

def _segment_sum(src, seg, n):
    return jax.ops.segment_sum(src, seg, n)
kernel_name = 'mk_prb_d2_jaxref_r8_6a1397'

def setup_inputs(seed: int=0):
    np.random.seed(seed)
    _w = jnp.asarray

    def _L0_attn_setup():
        import math
        import jax, jax.numpy as jnp
        import numpy as np
        DIM = 128
        N_HEADS = 16
        N_KV_HEADS = 4
        HEAD_DIM = 64
        WINDOW = 64
        EPS = 1e-06
        B, S = (2, 256)

        def _alibi_slopes(n_heads):

            def pow2(n):
                r = 2.0 ** (-8.0 / n)
                return np.array([r ** (i + 1) for i in range(n)], dtype=np.float32)
            if math.log2(n_heads).is_integer():
                return pow2(n_heads)
            m = 2 ** math.floor(math.log2(n_heads))
            return np.concatenate([pow2(m), pow2(2 * m)[::2][:n_heads - m]])

        def _rmsnorm(x, w, eps=EPS):
            var = jnp.mean(x * x, axis=-1, keepdims=True)
            return x * jax.lax.rsqrt(var + eps) * w
        key = jax.random.key(seed)
        ks = jax.random.split(key, 8)
        x = jax.random.normal(ks[0], (B, S, DIM), dtype=jnp.float32)
        wq = 0.02 * jax.random.normal(ks[1], (N_HEADS * HEAD_DIM, DIM), dtype=jnp.float32)
        wk = 0.02 * jax.random.normal(ks[2], (N_KV_HEADS * HEAD_DIM, DIM), dtype=jnp.float32)
        wv = 0.02 * jax.random.normal(ks[3], (N_KV_HEADS * HEAD_DIM, DIM), dtype=jnp.float32)
        wo = 0.02 * jax.random.normal(ks[4], (DIM, N_HEADS * HEAD_DIM), dtype=jnp.float32)
        q_norm_w = jnp.ones((N_HEADS * HEAD_DIM,), dtype=jnp.float32)
        k_norm_w = jnp.ones((N_KV_HEADS * HEAD_DIM,), dtype=jnp.float32)
        return {'x': x, 'wq': wq, 'wk': wk, 'wv': wv, 'wo': wo, 'q_norm_w': q_norm_w, 'k_norm_w': k_norm_w}
    _L0_attn_in = _L0_attn_setup()

    def _L0_ffn_setup():
        import jax, jax.numpy as jnp
        import numpy as np
        LN_EPS = 0.001
        EPS = 1e-05
        QB = 128.0

        def ste_round(x):
            return x + jax.lax.stop_gradient(jnp.round(x) - x)
        key = jax.random.key(seed)
        k1, k2 = jax.random.split(key)
        x = jax.random.normal(k1, (4, 1024, 128), dtype=jnp.float32)
        weight = jax.random.normal(k2, (128, 128), dtype=jnp.float32) * 0.02
        ln_gamma = jnp.ones((128,), dtype=jnp.float32)
        ln_beta = jnp.zeros((128,), dtype=jnp.float32)
        return {'x': x, 'weight': weight, 'ln_gamma': ln_gamma, 'ln_beta': ln_beta}
    _L0_ffn_in = _L0_ffn_setup()

    def _L1_attn_setup():
        import math
        import jax, jax.numpy as jnp
        import numpy as np
        N_HEADS = 16
        D_EMBED = 128
        key = jax.random.key(seed)
        ks = jax.random.split(key, 5)
        b, l, d = (2, 256, D_EMBED)
        return {'x': jax.random.normal(ks[0], (b, l, d), dtype=jnp.float32), 'w_in': jax.random.normal(ks[1], (3 * d, d), dtype=jnp.float32) * 0.02, 'b_in': jax.random.normal(ks[2], (3 * d,), dtype=jnp.float32) * 0.02, 'w_out': jax.random.normal(ks[3], (d, d), dtype=jnp.float32) * 0.02, 'b_out': jax.random.normal(ks[4], (d,), dtype=jnp.float32) * 0.02}
    _L1_attn_in = _L1_attn_setup()

    def _L1_ffn_setup():
        import jax, jax.numpy as jnp
        import numpy as np
        D_MODEL = 128
        D_FF = 512
        NUM_EXPERTS = 8
        B, N = (16, 128)
        key = jax.random.key(seed)
        ks = jax.random.split(key, 7)
        s_in = 1.0 / np.sqrt(D_MODEL)
        s_ff = 1.0 / np.sqrt(D_FF)
        return {'x': jax.random.normal(ks[0], (B, N, D_MODEL), dtype=jnp.float32), 'Wr': jax.random.uniform(ks[1], (D_MODEL, NUM_EXPERTS), jnp.float32, -s_in, s_in), 'br': jax.random.uniform(ks[2], (NUM_EXPERTS,), jnp.float32, -s_in, s_in), 'W1': jax.random.uniform(ks[3], (NUM_EXPERTS, D_MODEL, D_FF), jnp.float32, -s_in, s_in), 'b1': jax.random.uniform(ks[4], (NUM_EXPERTS, D_FF), jnp.float32, -s_in, s_in), 'W2': jax.random.uniform(ks[5], (NUM_EXPERTS, D_FF, D_MODEL), jnp.float32, -s_ff, s_ff), 'b2': jax.random.uniform(ks[6], (NUM_EXPERTS, D_MODEL), jnp.float32, -s_ff, s_ff)}
    _L1_ffn_in = _L1_ffn_setup()
    _d = {'L0_attn_x': _L0_attn_in['x'], 'L0_attn_wq': _L0_attn_in['wq'], 'L0_attn_wk': _L0_attn_in['wk'], 'L0_attn_wv': _L0_attn_in['wv'], 'L0_attn_wo': _L0_attn_in['wo'], 'L0_attn_q_norm_w': _L0_attn_in['q_norm_w'], 'L0_attn_k_norm_w': _L0_attn_in['k_norm_w'], 'L0_ffn_weight': _L0_ffn_in['weight'], 'L0_ffn_ln_gamma': _L0_ffn_in['ln_gamma'], 'L0_ffn_ln_beta': _L0_ffn_in['ln_beta'], 'L1_attn_w_in': _L1_attn_in['w_in'], 'L1_attn_b_in': _L1_attn_in['b_in'], 'L1_attn_w_out': _L1_attn_in['w_out'], 'L1_attn_b_out': _L1_attn_in['b_out'], 'L1_ffn_Wr': _L1_ffn_in['Wr'], 'L1_ffn_br': _L1_ffn_in['br'], 'L1_ffn_W1': _L1_ffn_in['W1'], 'L1_ffn_b1': _L1_ffn_in['b1'], 'L1_ffn_W2': _L1_ffn_in['W2'], 'L1_ffn_b2': _L1_ffn_in['b2']}
    _x0 = _d['L0_attn_x']
    _d['L0_attn_x'] = jax.random.normal(jax.random.fold_in(jax.random.key(seed), 1), (1, 2048, 128), dtype=_x0.dtype)
    del _x0
    return _d

def reference(L0_attn_x, L0_attn_wq, L0_attn_wk, L0_attn_wv, L0_attn_wo, L0_attn_q_norm_w, L0_attn_k_norm_w, L0_ffn_weight, L0_ffn_ln_gamma, L0_ffn_ln_beta, L1_attn_w_in, L1_attn_b_in, L1_attn_w_out, L1_attn_b_out, L1_ffn_Wr, L1_ffn_br, L1_ffn_W1, L1_ffn_b1, L1_ffn_W2, L1_ffn_b2):

    def _L0_attn_ref(x, wq, wk, wv, wo, q_norm_w, k_norm_w):
        import math
        import jax, jax.numpy as jnp
        import numpy as np
        DIM = 128
        N_HEADS = 16
        N_KV_HEADS = 4
        HEAD_DIM = 64
        WINDOW = 64
        EPS = 1e-06
        B, S = (2, 256)

        def _alibi_slopes(n_heads):

            def pow2(n):
                r = 2.0 ** (-8.0 / n)
                return np.array([r ** (i + 1) for i in range(n)], dtype=np.float32)
            if math.log2(n_heads).is_integer():
                return pow2(n_heads)
            m = 2 ** math.floor(math.log2(n_heads))
            return np.concatenate([pow2(m), pow2(2 * m)[::2][:n_heads - m]])

        def _rmsnorm(x, w, eps=EPS):
            var = jnp.mean(x * x, axis=-1, keepdims=True)
            return x * jax.lax.rsqrt(var + eps) * w
        bsz, seqlen, _ = x.shape
        repeats = N_HEADS // N_KV_HEADS
        xq = _rmsnorm(x @ wq.T, q_norm_w)
        xk = _rmsnorm(x @ wk.T, k_norm_w)
        xv = x @ wv.T
        q = xq.reshape(bsz, seqlen, N_HEADS, HEAD_DIM).transpose(0, 2, 1, 3)
        k = xk.reshape(bsz, seqlen, N_KV_HEADS, HEAD_DIM).transpose(0, 2, 1, 3)
        v = xv.reshape(bsz, seqlen, N_KV_HEADS, HEAD_DIM).transpose(0, 2, 1, 3)
        k = jnp.repeat(k, repeats, axis=1)
        v = jnp.repeat(v, repeats, axis=1)
        pos = jnp.arange(seqlen)
        rel = pos[None, :] - pos[:, None]
        slopes = jnp.asarray(_alibi_slopes(N_HEADS))
        bias = slopes[:, None, None] * rel[None].astype(x.dtype)
        masked = (rel > 0) | (rel < -WINDOW)
        bias = jnp.where(masked[None], -jnp.inf, bias)
        scale = 1.0 / math.sqrt(HEAD_DIM)
        scores = jnp.einsum('bhqd,bhkd->bhqk', q, k) * scale + bias[None]
        probs = jax.nn.softmax(scores, axis=-1)
        y = jnp.einsum('bhqk,bhkd->bhqd', probs, v)
        y = y.transpose(0, 2, 1, 3).reshape(bsz, seqlen, N_HEADS * HEAD_DIM)
        return y @ wo.T

    def _L0_ffn_ref(x, weight, ln_gamma, ln_beta):
        import jax, jax.numpy as jnp
        import numpy as np
        LN_EPS = 0.001
        EPS = 1e-05
        QB = 128.0

        def ste_round(x):
            return x + jax.lax.stop_gradient(jnp.round(x) - x)
        mu = jnp.mean(x, axis=-1, keepdims=True)
        var = jnp.var(x, axis=-1, keepdims=True)
        xn = (x - mu) * jax.lax.rsqrt(var + LN_EPS) * ln_gamma + ln_beta
        beta = jnp.mean(jnp.abs(weight))
        w_q = jnp.clip(ste_round(weight / (beta + EPS)), -1.0, 1.0)
        gamma = jnp.max(jnp.abs(xn))
        xq = jnp.clip(xn * QB / gamma, -QB + EPS, QB - EPS)
        y = jnp.einsum('bsd,du->bsu', xq, w_q)
        return y * (gamma * beta / QB)

    def _L1_attn_ref(x, w_in, b_in, w_out, b_out):
        import math
        import jax, jax.numpy as jnp
        import numpy as np
        N_HEADS = 16
        D_EMBED = 128
        b, l, d = x.shape
        h = N_HEADS
        scale = 1.0 / math.sqrt(d // h)
        x_proj = (x @ w_in.T + b_in).reshape(b, l, h, -1)
        q, k, v = jnp.split(x_proj, 3, axis=-1)
        att = jnp.einsum('blhd,bmhd->blmh', q, k) * scale
        att = jax.nn.softmax(att, axis=2)
        opt = jnp.einsum('blmh,blhd->blhd', att, v).reshape(b, l, d)
        return opt @ w_out.T + b_out

    def _L1_ffn_ref(x, Wr, br, W1, b1, W2, b2):
        import jax, jax.numpy as jnp
        import numpy as np
        D_MODEL = 128
        D_FF = 512
        NUM_EXPERTS = 8
        B, N = (16, 128)
        scores = jnp.einsum('bh,he->be', x.mean(axis=1), Wr) + br
        top1 = jnp.argmax(scores, axis=-1)
        w1 = W1[top1]
        c1 = b1[top1]
        w2 = W2[top1]
        c2 = b2[top1]
        h = jax.nn.relu(jnp.einsum('bnh,bhf->bnf', x, w1) + c1[:, None, :])
        out = jnp.einsum('bnf,bfh->bnh', h, w2) + c2[:, None, :]
        return out
    x = L0_attn_x
    xn = _layernorm(x, axis=-1)
    x = x + _L0_attn_ref(xn, L0_attn_wq, L0_attn_wk, L0_attn_wv, L0_attn_wo, L0_attn_q_norm_w, L0_attn_k_norm_w) + _L0_ffn_ref(xn, L0_ffn_weight, L0_ffn_ln_gamma, L0_ffn_ln_beta)
    xn = _layernorm(x, axis=-1)
    x = x + _L1_attn_ref(xn, L1_attn_w_in, L1_attn_b_in, L1_attn_w_out, L1_attn_b_out) + _L1_ffn_ref(xn, L1_ffn_Wr, L1_ffn_br, L1_ffn_W1, L1_ffn_b1, L1_ffn_W2, L1_ffn_b2)
    return x

_drawn_inputs = setup_inputs


def setup_inputs(seed=0):
    import zlib

    import numpy as np

    out = dict(_drawn_inputs(seed))
    spreads = {'L0_attn_q_norm_w': (1.0, 0.6),
     'L0_attn_k_norm_w': (1.0, 0.6),
     'L0_ffn_ln_gamma': (1.0, 0.2),
     'L0_ffn_ln_beta': (0.0, 0.52)}
    factors = {'L1_attn_b_in': 8.0, 'L1_attn_b_out': 2.899, 'L1_ffn_b1': 3.192}
    for name, (base, spread) in spreads.items():
        noise = np.random.default_rng([zlib.crc32(name.encode()), seed]).standard_normal(out[name].shape)
        drawn = base * np.exp(spread * noise) if base else spread * noise
        out[name] = jnp.asarray(drawn.astype(out[name].dtype))
    for name, factor in factors.items():
        out[name] = (out[name] * factor).astype(out[name].dtype)
    return out
```

```python
from contextlib import ExitStack

import concourse.bass as bass
from concourse import mybir

F32 = mybir.dt.float32
BF16 = mybir.dt.bfloat16
U32 = mybir.dt.uint32
ALU = mybir.AluOpType
ACT = mybir.ActivationFunctionType
AX = mybir.AxisListType
RMAX = bass.bass_isa.ReduceOp.max

P = 128
C = 128
HEADS, KV, HD = 16, 4, 64
BLK = 64
WIN = P + BLK
CH = HEADS * HD // P
H1, D1 = 16, 8
PAIRS = ((0, 0), (0, 1), (0, 2), (1, 0), (1, 1), (2, 0))
ROWS = len(PAIRS) * D1
QUART = 512
CHUNKS = [(h, s, (2 * s, 2 * s + 1)) for h in range(15) for s in range(2)] + [
    (15, 0, (0, 1)), (15, 1, (2,)), (15, 2, (3,))]
NC, NS, BUFS = len(CHUNKS), 3, 3
EXPERTS, FF = 8, 512
FC = FF // P
BIG = -1e30
ROUND = 1.5 * 2.0 ** 23
LIM = 128.0 - 1e-5


def head_of(cph, r, j):
    return cph * 8 + r * 4 + j


def two_layers(nc, x, wq, wk, wv, wo, q_norm_w, k_norm_w, ffn_w, ln_gamma, ln_beta,
               w_in, b_in, w_out, b_out, Wr, br, W1, b1, W2, b2, alibi, out):
    _, S, _ = x.shape
    T = S // P
    NQ = S // QUART
    TQ = QUART // P

    with ExitStack() as ctx:
        def sb(name, shape, dt=F32):
            return ctx.enter_context(nc.sbuf_tensor(name, shape, dt))

        def sem(name):
            return ctx.enter_context(nc.semaphore(name))

        ps = ctx.enter_context(nc.psum_tensor("ps", [P, 8, 512], F32))

        ident = sb("ident", [P, P])
        ones = sb("ones", [P, P])
        cst = sb("cst", [P, 8])
        rows = sb("rows", [12, P])
        rowsT = sb("rowsT", [P, 12])
        w_kv = sb("w_kv", [P, 4, C])
        wk_s = sb("wk_s", [P, 2, C])
        gram = sb("gram", [P, 2, C])
        wqT = sb("wqT", [C, CH, P])
        wkvT = sb("wkvT", [C, 4, P])
        woT = sb("woT", [P, CH, C])
        tern = sb("tern", [C, C])
        w_inT = sb("w_inT", [C, 3, D1, H1])
        w_outT = sb("w_outT", [P, C])
        bin_nat = sb("bin_nat", [1, 3 * C])
        bin_row = sb("bin_row", [1, 3, D1, H1])
        outb = sb("outb", [2, C])
        c1row = sb("c1row", [1, FF])
        wr_s = sb("wr_s", [C, EXPERTS])
        br_s = sb("br_s", [1, EXPERTS])
        gate = sb("gate", [1, 3, EXPERTS])
        gidx = sb("gidx", [1, EXPERTS], U32)
        xsum = sb("xsum", [C, T + 1])
        st = sb("st", [P, T, 6])
        mv = sb("mv", [P, T, 2])
        rstd = sb("rstd", [P, T])
        st2 = sb("st2", [P, T, 6])
        mv2 = sb("mv2", [P, T, 2])
        rstd2 = sb("rstd2", [P, T])
        st3 = sb("st3", [P, 2, 6])
        mv3 = sb("mv3", [P, 2, 2])
        rstd3 = sb("rstd3", [P, 2])
        fsc = sb("fsc", [P, 16])
        xs = sb("xs", [P, T, C])
        x1 = sb("x1", [P, T, C])
        xnT = sb("xnT", [C, BLK + S])
        xkT = sb("xkT", [C, BLK + S])
        xqf = sb("xqf", [C, 2, S])
        xqT, xfT = xqf[:, 0, :], xqf[:, 1, :]
        biasm = sb("biasm", [P, 8, P])
        qs = sb("qs", [P, 2, CH, P])
        ks = sb("ks", [P, 2, 2, WIN])
        vs = sb("vs", [P, 2, 2, 2 * C])
        win = sb("win", [C, 2, WIN])
        ffx = sb("ffx", [C, 2, 2, P])
        sp = sb("sp", [P, 2, 16, P])
        z0 = sb("z0", [P, 2, 3, 16])
        pTs = sb("pTs", [P, 2, 8, P])
        yTs = sb("yTs", [P, 2, CH, P])
        xn1 = sb("xn1", [P, 2, C])
        xn1T = sb("xn1T", [C, S])
        vT = sb("vT", [P, S])
        rem = sb("rem", [P, 2, 2, P])
        parts = sb("parts", [P, 2, 3, 2, P], BF16)
        kst = sb("kst", [ROWS, 3, H1, QUART], BF16)
        fT = sb("fT", [P, 6, NS * H1])
        frep = sb("frep", [P, P])
        lnm = sb("lnm", [P, T, NS * H1])
        lz = sb("lz", [P, T, NS * H1])
        optT = sb("optT", [P, P])

        wq_nat = pTs[:].rearrange("p a b c -> p (a b) c")[:, 0:CH, :]
        wq_s = pTs[:].rearrange("p a b c -> p (a b) c")[:, CH:2 * CH, :]
        wo_nat = yTs[:, 0].rearrange("p a (r d) -> p a r d", r=2)
        w_nat = xn1T[:, 0:4 * C].rearrange("p (a c) -> p a c", a=4)
        xn2 = sp[:, 0]
        gx = sp[:, 1].rearrange("p a b -> p (a b)").rearrange("p (k n) -> p k n", k=4)
        kst3 = xqf[:].rearrange("p a b -> p (a b)").bitcast(BF16).rearrange("p (h n) -> p h n", h=H1)
        qst = xnT[:, 0:S].bitcast(BF16).rearrange("p (h n) -> p h n", n=P)[:, 0:H1, :]
        w1e = xkT[:, 0:FF]
        w2e = xkT[:, FF:2 * FF].rearrange("p (f c) -> p f c", f=FC)
        hT = xkT[:, 2 * FF:3 * FF].rearrange("p (f c) -> p f c", f=FC)

        scr_k = nc.dram_tensor("scr_k", [3, P, S], BF16, kind="Internal").ap()
        scr_q = nc.dram_tensor("scr_q", [len(PAIRS), P, S], BF16, kind="Internal").ap()

        x_in = [sem(f"x_in{c}") for c in range(NQ)]
        wa_in, wb_in, bias_in = sem("wa_in"), sem("wb_in"), sem("bias_in")
        consts = sem("consts")
        dve_pro, pool_pro, act_pro, pe_pro = sem("dve_pro"), sem("pool_pro"), sem("act_pro"), sem("pe_pro")
        xn_ready, xn2_ready, xnT_done, xn_copied, xfT_done, xf_copied = (
            sem("xn_ready"), sem("xn2_ready"), sem("xnT_done"), sem("xn_copied"), sem("xfT_done"), sem("xf_copied"))
        gx_done, gx_ready, ssq_done, act_mean, rms_ready, xqk_ready = (
            sem("gx_done"), sem("gx_ready"), sem("ssq_done"), sem("act_mean"), sem("rms_ready"), sem("xqk_ready"))
        amax_ready, gmax_ready, fsc_ready, wabs_ready, tern_step, wqk_scaled, first_masked = (
            sem("amax_ready"), sem("gmax_ready"), sem("fsc_ready"), sem("wabs_ready"), sem("tern_step"),
            sem("wqk_scaled"), sem("first_masked"))
        win_ready, ffx_ready = sem("win_ready"), sem("ffx_ready")
        q_done, kv_done = sem("q_done"), sem("kv_done")
        q_copied, v_copied, k_copied = sem("q_copied"), sem("v_copied"), sem("k_copied")
        scores_done, bias_added, nmax_ready, exp_done = (
            sem("scores_done"), sem("bias_added"), sem("nmax_ready"), sem("exp_done"))
        rz_ready, probs_ready = sem("rz_ready"), sem("probs_ready")
        pT_done, pTa_copied, pTd_copied = sem("pT_done"), sem("pTa_copied"), sem("pTd_copied")
        y_done, ya_copied, yd_copied = sem("y_done"), sem("ya_copied"), sem("yd_copied")
        x1_done, x1_ready, st_ready, mv_ready, rstd_ready, xn1_ready = (
            sem("x1_done"), sem("x1_ready"), sem("st_ready"), sem("mv_ready"), sem("rstd_ready"), sem("xn1_ready"))
        xT_done, xn1T_copied, qkv_done = sem("xT_done"), sem("xn1T_copied"), sem("qkv_done")
        p1_ready, rem_ready, p2_ready, split_ready = (
            sem("p1_ready"), sem("rem_ready"), sem("p2_ready"), sem("split_ready"))
        scr_w = [sem("scr_w0"), sem("scr_w1")]
        kst_in = [sem(f"kst_in{q}") for q in range(NQ)]
        ffx_step = sem("ffx_step")
        gate_step, gate_pe, exp_in = sem("gate_step"), sem("gate_pe"), sem("exp_in")
        q_in = [sem("q_in0"), sem("q_in1")]
        l_scores, l_max, l_slots = sem("l_scores"), sem("l_max"), sem("l_slots")
        mn_ready, h_ready, chunks_set = sem("mn_ready"), sem("h_ready"), sem("chunks_set")
        h_done, comb, comb_e, f_done, opt_ready, o_done, o_ready, stored = (
            sem("h_done"), sem("comb"), sem("comb_e"), sem("f_done"), sem("opt_ready"), sem("o_done"),
            sem("o_ready"), sem("stored"))

        block = ctx.enter_context(nc.Block())

        def tiles(eng, step, lag):
            for t in range(4):
                step(t, t % 2)
            with eng.Fori(2, T // 2) as i:
                for u in (0, 1):
                    step(i * 2 + u, u)
            for t in range(T, T + lag):
                step(t, t % 2)

        def has(t, lag=0):
            return not isinstance(t, int) or 0 <= t - lag < T

        def later(t, n=0):
            return not isinstance(t, int) or t - n > 0

        def tok(t):
            return bass.ds(t * P, P)

        NWA, NWB = 11, 13

        @block.sync
        def _(sp_):
            xv = x.rearrange("a (c t p) d -> (a c) p t d", c=NQ, p=P)
            for c in range(NQ):
                sp_.dma_start(xs[:, c * TQ:(c + 1) * TQ, :], xv[c]).then_inc(x_in[c], 16)
            sp_.dma_start(biasm[:], alibi).then_inc(bias_in, 16)

            def write_parts(t, u):
                sp_.wait_ge(split_ready, t + 1)
                sp_.dma_start(scr_k[:, :, tok(t)].rearrange("j p n -> p j n"),
                              parts[:, u, :, 1, :]).then_inc(scr_w[u], 16)
                for i, (a, n) in enumerate(((0, 3), (3, 2), (5, 1))):
                    sp_.dma_start(scr_q[a:a + n, :, tok(t)].rearrange("j p n -> p j n"),
                                  parts[:, u, i:i + 1, 0, :].broadcast_to([P, n, P])).then_inc(scr_w[u], 16)

            def read_keys(q, dst, signal):
                for u in (0, 1):
                    sp_.wait_ge(scr_w[u], (q * (TQ // 2) + TQ // 2) * 64)
                src = scr_k.rearrange("j (d h) n -> (j d) h n", h=H1)
                for a, n in ((0, 3), (3, 2), (5, 1)):
                    sp_.dma_start(dst[a * D1:(a + n) * D1], src[0:n * D1, :, bass.ds(q * QUART, QUART)]
                                  ).then_inc(signal, 16)

            with sp_.Fori(0, NQ - 1) as q:
                for j in range(TQ):
                    write_parts(q * TQ + j, j % 2)
                read_keys(q, kst[:, bass.ds(q, 1)].rearrange("p a h n -> p (a h) n"), kst_in[0])
            for j in range(TQ):
                write_parts((NQ - 1) * TQ + j, j % 2)
            sp_.wait_ge(q_done, T)
            sp_.wait_ge(ffx_ready, T)
            read_keys(NQ - 1, kst3[0:ROWS], kst_in[3])

            qsrc = scr_q.rearrange("j (d h) n -> (j d) h n", h=H1)
            sp_.wait_ge(win_ready, T)

            def read_q(t, g):
                hs = slice(g * 8, g * 8 + 8)
                sp_.dma_start(qst[0:ROWS, hs, :], qsrc[:, hs, tok(t)]).then_inc(q_in[g], 16)

            read_q(0, 0)
            read_q(0, 1)
            sp_.wait_ge(kv_done, T)
            sp_.wait_ge(gate_step, 4)
            e = sp_.value_load(gidx[0:1, 0:1], min_val=0, max_val=EXPERTS - 1)
            sp_.dma_start(w1e, W1[bass.ds(e, 1)].rearrange("e c f -> (e c) f")).then_inc(exp_in, 16)
            sp_.dma_start(c1row[:], b1[bass.ds(e, 1), :]).then_inc(exp_in, 16)
            sp_.dma_start(w2e, W2[bass.ds(e, 1)].rearrange("e (f p) c -> p (e f) c", p=P)).then_inc(exp_in, 16)
            sp_.dma_start(outb[1:2, :], b2[bass.ds(e, 1), :]).then_inc(exp_in, 16)
            ov = out.rearrange("a (t p) d -> (a t) p d", p=P)
            with sp_.Fori(1, T) as t:
                sp_.wait_ge(l_scores, t * NC - (NC - 16))
                read_q(t, 0)
                sp_.wait_ge(l_scores, t * NC)
                read_q(t, 1)
                sp_.wait_ge(o_ready, t)
                sp_.dma_start(ov[bass.ds(t - 1, 1)].rearrange("a p d -> p (a d)"),
                              x1[:, bass.ds(t - 1, 1), :].rearrange("p a d -> p (a d)")).then_inc(stored, 16)
            sp_.wait_ge(o_ready, T)
            sp_.dma_start(ov[T - 1], x1[:, T - 1, :]).then_inc(stored, 16)
            sp_.wait_ge(stored, 16 * T)

        @block.gpsimd
        def _(pool):
            pool.memset(ident[:], 0.0).then_inc(consts, 1)
            pool.memset(ones[:], 1.0).then_inc(consts, 1)
            pool.memset(cst[:, 0:1], -0.5).then_inc(consts, 1)
            pool.memset(cst[:, 1:2], -1.0).then_inc(consts, 1)
            pool.memset(cst[:, 2:3], 1e-6).then_inc(consts, 1)
            pool.memset(cst[:, 3:4], 0.0).then_inc(consts, 1)
            pool.memset(lnm[:], -BIG).then_inc(chunks_set, 1)
            pool.memset(lz[:], 0.0).then_inc(chunks_set, 1)
            pool.wait_ge(consts, 6)
            pool.affine_select(out=ident[:], in_=ident[:], compare_op=ALU.not_equal, fill=1.0, base=0,
                               pattern=[[-1, P]], channel_multiplier=1).then_inc(consts, 1)
            pool.memset(xnT[:, 0:BLK], 0.0).then_inc(consts, 1)
            pool.memset(xkT[:, 0:BLK], 0.0).then_inc(consts, 1)
            pool.wait_ge(consts, 9)

            def power(o, i, col, n):
                return pool.tensor_tensor(o, i, cst[:, col:col + 1].broadcast_to([P, n]), ALU.pow)

            for c in range(NQ):
                ts = slice(c * TQ, (c + 1) * TQ)
                pool.wait_ge(dve_pro, 20 * c + 12)
                power(rstd[:, ts], mv[:, ts, 1], 0, TQ).then_inc(pool_pro, 1)
                pool.wait_ge(dve_pro, 20 * c + 20)
                power(rstd2[:, ts], mv2[:, ts, 1], 0, TQ).then_inc(pool_pro, 1)
            pool.wait_ge(amax_ready, NQ + 1)
            pool.partition_all_reduce(fsc[:, 6:7], fsc[:, 5:6], P, RMAX).then_inc(gmax_ready, 1)

            def window(t, u):
                if later(t, 1):
                    pool.wait_ge(kv_done, t - 1)
                pool.tensor_tensor(win[:, u, :], xnT[:, bass.ds(t * P, WIN)], cst[:, 3:4].broadcast_to([P, WIN]),
                                   ALU.add).then_inc(win_ready, 1)

            pool.wait_ge(xn_copied, NQ)
            window(0, 0)

            def step(t, u):
                v = 1 - u
                if has(t, -1) and (not isinstance(t, int) or t + 1 < T):
                    window(t + 1, v)
                if has(t, 2):
                    pool.wait_ge(mv_ready, (t - 1) * 2)
                    power(rstd3[:, u:u + 1], mv3[:, u, 1:2], 0, 1).then_inc(rstd_ready, 1)

                def normalize(h):
                    hs = slice(8 * h, 8 * h + 8)
                    pool.wait_ge(exp_done, t * 2 + h + 1)
                    power(z0[:, u, 2, hs], z0[:, u, 1, hs], 1, 8).then_inc(rz_ready, 1)
                    pool.wait_ge(rz_ready, t * 2 + h + 1)
                    pool.tensor_tensor(sp[:, u, hs, :], sp[:, u, hs, :],
                                       z0[:, u, 2, hs].unsqueeze(2).broadcast_to([P, 8, P]),
                                       ALU.mult).then_inc(probs_ready, 1)

                if has(t):
                    normalize(0)
                if has(t, 2):
                    pool.wait_ge(rem_ready, t - 1)
                    pool.tensor_tensor(parts[:, u, 1], rem[:, u], cst[:, 3:4].unsqueeze(2).broadcast_to([P, 2, P]),
                                       ALU.add).then_inc(p2_ready, 1)
                    pool.wait_ge(p2_ready, t - 1)
                    pool.tensor_tensor(parts[:, u, 2], rem[:, u], parts[:, u, 1],
                                       ALU.subtract).then_inc(split_ready, 1)
                if has(t):
                    normalize(1)

            for t in range(4):
                step(t, t % 2)
            with pool.Fori(2, T // 2 - 1) as i:
                for u in (0, 1):
                    step(i * 2 + u, u)
            for t in range(T - 2, T + 2):
                step(t, t % 2)

            def combine(t):
                m = lnm[:, bass.ds(t, 1), :].rearrange("p a (h s) -> p (a h) s", s=NS)
                z = lz[:, bass.ds(t, 1), :].rearrange("p a (h s) -> p (a h) s", s=NS)
                d, e, w = (fT[:, k, :].rearrange("p (h s) -> p h s", s=NS) for k in range(1, 4))
                n = t * 6
                pool.wait_ge(l_slots, (t + 1) * NC)
                pool.wait_ge(mn_ready, t + 1)
                pool.tensor_tensor(d, fT[:, 0, 0:H1].unsqueeze(2).broadcast_to([P, H1, NS]), m,
                                   ALU.subtract).then_inc(comb, 1)
                pool.wait_ge(comb_e, t + 1)
                pool.tensor_tensor(w, z, e, ALU.mult).then_inc(comb, 1)
                pool.wait_ge(comb, n + 2)
                pool.tensor_tensor(fT[:, 4, 0:H1], w[:, :, 0], w[:, :, 1], ALU.add).then_inc(comb, 1)
                pool.wait_ge(comb, n + 3)
                pool.tensor_tensor(fT[:, 4, H1:2 * H1], fT[:, 4, 0:H1], w[:, :, 2], ALU.add).then_inc(comb, 1)
                pool.wait_ge(comb, n + 4)
                power(fT[:, 5, 0:H1], fT[:, 4, H1:2 * H1], 1, H1).then_inc(comb, 1)
                pool.wait_ge(comb, n + 5)
                pool.tensor_tensor(frep[:].rearrange("p (d h) -> p d h", d=D1),
                                   fT[:, 4:5, H1:2 * H1].broadcast_to([P, D1, H1]),
                                   fT[:, 5:6, 0:H1].broadcast_to([P, D1, H1]), ALU.mult).then_inc(comb, 1)

            with pool.Fori(0, T) as t:
                combine(t)

        @block.scalar
        def _(act):
            r_of = lambda r: slice(r * HD, (r + 1) * HD)
            wqv = wq.rearrange("(cph r j d) c -> r d cph j c", cph=2, r=2, j=4)
            wov = wo.rearrange("o (cph r j d) -> o cph r j d", cph=2, r=2, j=4)
            qnv = q_norm_w.rearrange("(cph r j d) -> cph r j d", cph=2, r=2, j=4)
            for cph in (0, 1):
                for r in (0, 1):
                    act.dma_start(wq_nat[r_of(r), cph * 4:cph * 4 + 4, :], wqv[r, :, cph]).then_inc(wa_in, 16)
            act.dma_start(w_kv[:, 0:2, :], wk.rearrange("(a p) c -> p a c", p=P)).then_inc(wa_in, 16)
            act.dma_start(w_kv[:, 2:4, :], wv.rearrange("(a p) c -> p a c", p=P)).then_inc(wa_in, 16)
            for cph in (0, 1):
                for r in (0, 1):
                    act.dma_start(rows[cph * 4:cph * 4 + 4, r_of(r)], qnv[cph, r]).then_inc(wa_in, 16)
            act.dma_start(rows[8:10, :], k_norm_w.rearrange("(a p) -> a p", p=P)).then_inc(wa_in, 16)
            act.dma_start(rows[10:11, :], ln_gamma.unsqueeze(0)).then_inc(wb_in, 16)
            act.dma_start(rows[11:12, :], ln_beta.unsqueeze(0)).then_inc(wb_in, 16)
            for cph in (0, 1):
                for r in (0, 1):
                    act.dma_start(wo_nat[:, cph * 4:cph * 4 + 4, r, :], wov[:, cph, r]).then_inc(wb_in, 16)
            act.dma_start(tern[:], ffn_w).then_inc(wb_in, 16)
            act.dma_start(w_nat[:, 0:3, :], w_in.rearrange("(a p) c -> p a c", p=P)).then_inc(wb_in, 16)
            act.dma_start(w_nat[:, 3, :], w_out).then_inc(wb_in, 16)
            act.dma_start(bin_nat[:], b_in.unsqueeze(0)).then_inc(wb_in, 16)
            act.dma_start(outb[0:1, :], b_out.unsqueeze(0)).then_inc(wb_in, 16)
            act.dma_start(wr_s[:], Wr).then_inc(wb_in, 16)
            act.dma_start(br_s[:], br.unsqueeze(0)).then_inc(wb_in, 16)

            def copy(o, i, signal, **kw):
                return act.activation(o, i, ACT.Identity, **kw).then_inc(signal, 1)

            bank = lambda b, n=1: ps[:, b:b + n, :].rearrange("p b n -> p (b n)")
            act.wait_ge(pe_pro, 1)
            copy(rowsT[:], ps[:, 7, 0:12], act_pro)
            act.wait_ge(pe_pro, 2)
            copy(gram[:], ps[:, 6, 0:2 * C].rearrange("p (a c) -> p a c", a=2), act_pro)
            act.wait_ge(pe_pro, 3)
            copy(wqT[:].rearrange("p a b -> p (a b)"), bank(0, 2), act_pro, scale=HD ** -0.5)
            act.wait_ge(pe_pro, 4)
            copy(wkvT[:].rearrange("p a b -> p (a b)"), bank(2), act_pro)
            act.wait_ge(pe_pro, 5)
            copy(woT[:].rearrange("p a b -> p (a b)"), bank(3, 2), act_pro)
            act.wait_ge(pe_pro, 6)
            win_v = ps[:, 5, 0:3 * C].rearrange("p (h s d) -> p s d h", s=3, d=D1)
            act.activation(w_inT[:, 0], win_v[:, 0], ACT.Identity, scale=D1 ** -0.5)
            act.activation(w_inT[:, 1], win_v[:, 1], ACT.Identity)
            act.activation(w_inT[:, 2], win_v[:, 2], ACT.Identity)
            copy(w_outT[:], ps[:, 5, 3 * C:4 * C], act_pro)
            bin_v = bin_nat[:].rearrange("p (h s d) -> p s d h", s=3, d=D1)
            act.activation(bin_row[:, 0], bin_v[:, 0], ACT.Identity, scale=D1 ** -0.5)
            act.activation(bin_row[:, 1], bin_v[:, 1], ACT.Identity)
            copy(bin_row[:, 2], bin_v[:, 2], act_pro)
            for c in range(NQ):
                act.wait_ge(xnT_done, c + 1)
                copy(xnT[:, BLK + c * QUART:BLK + (c + 1) * QUART], bank(c % 2), xn_copied)
                act.wait_ge(xfT_done, c + 1)
                if c == 0:
                    act.wait_ge(act_pro, 1)
                copy(xfT[:, c * QUART:(c + 1) * QUART], bank(7), xf_copied, scale=rowsT[:, 10:11],
                     bias=rowsT[:, 11:12])
                act.wait_ge(ssq_done, c + 1)
                if c:
                    act.wait_ge(xqk_ready, 2 * c)
                for k, n in ((0, HEADS * HD), (1, KV * HD)):
                    act.activation(gx[:, 2 + k, :], bank(4 + k), ACT.Sqrt, scale=1.0 / n,
                                   bias=cst[:, 2:3]).then_inc(act_mean, 1)

            def exps(t, u, a, b):
                for s in range(a, b):
                    last = act.activation(sp[:, u, s, :], sp[:, u, s, :], ACT.Exp, bias=z0[:, u, 0, s:s + 1],
                                          accum_out=z0[:, u, 1, s:s + 1])
                return last

            def copy_pT(t, h):
                act.wait_ge(pT_done, t * 2 + h + 1)
                if later(t):
                    act.wait_ge(y_done, t * 2 + h - 1)
                copy(pTs[:, h, 0:4, :].rearrange("p a b -> p (a b)"), bank(4), pTa_copied)

            def step(t, u):
                v = 1 - u
                if has(t):
                    act.wait_ge(q_done, t + 1)
                    if later(t, 1):
                        act.wait_ge(scores_done, (t - 1) * 2)
                    copy(qs[:, u].rearrange("p a b -> p (a b)"), bank(0, 2), q_copied)
                    act.wait_ge(kv_done, t + 1)
                    if later(t, 1):
                        act.wait_ge(y_done, (t - 1) * 2)
                    copy(vs[:, u].rearrange("p a b -> p (a b)"), bank(3), v_copied)
                if has(t, 1):
                    copy_pT(t - 1, 0)
                if has(t, 2):
                    act.wait_ge(xT_done, t - 1)
                    act.activation(xn1T[:, tok(t - 2)], ps[:, 7, 0:P], ACT.Identity,
                                   accum_out=xsum[:, bass.ds(t - 2, 1)]).then_inc(xn1T_copied, 1)
                if has(t, 1):
                    act.wait_ge(y_done, (t - 1) * 2 + 1)
                    if later(t - 1, 1):
                        act.wait_ge(x1_done, t - 2)
                    copy(yTs[:, v, 0:4, :].rearrange("p j (b q) -> p b j q", b=2),
                         ps[:, 6, :].rearrange("p (b j q) -> p b j q", b=2, j=4), ya_copied)
                if has(t):
                    act.wait_ge(nmax_ready, t * 2 + 1)
                    if later(t, 1):
                        act.wait_ge(probs_ready, (t - 1) * 2)
                    exps(t, u, 0, 4)
                if has(t, 1):
                    copy_pT(t - 1, 1)
                if has(t):
                    exps(t, u, 4, 8).then_inc(exp_done, 1)
                if has(t, 2):
                    act.wait_ge(qkv_done, t - 1)
                    act.activation(vT[:, tok(t - 2)], ps[:, 7, 3 * P:4 * P], ACT.Identity)
                    if later(t - 2, 1):
                        act.wait_ge(scr_w[u], (t - 2 - u) * 32)
                    copy(parts[:, u, 0].rearrange("p a b -> p (a b)"), ps[:, 7, P:3 * P], p1_ready)
                if has(t):
                    act.wait_ge(nmax_ready, t * 2 + 2)
                    exps(t, u, 8, 16).then_inc(exp_done, 1)

            tiles(act, step, 2)

            def combine_exp(t):
                act.wait_ge(comb, t * 6 + 1)
                act.activation(fT[:, 2, :], fT[:, 1, :], ACT.Exp).then_inc(comb_e, 1)

            def hidden(t):
                act.wait_ge(h_done, t + 1)
                if later(t):
                    act.wait_ge(o_done, t)
                act.activation(hT.rearrange("p a b -> p (a b)"), bank(6), ACT.Relu).then_inc(h_ready, 1)

            def attend(t, lagged):
                for k, (h, c, quarters) in enumerate(CHUNKS):
                    act.wait_ge(l_max, t * NC + k + 1)
                    b, n = 2 * (k % BUFS), len(quarters)
                    i = h * NS + c
                    col = lambda a: a[:, bass.ds(t, 1), i:i + 1].rearrange("p a b -> p (a b)")
                    act.activation(bank(b, n), bank(b, n), ACT.Exp, bias=col(lnm), accum_out=col(lz)
                                   ).then_inc(l_slots, 1)
                    if lagged and k == 2:
                        hidden(t - 1)
                    if lagged and k == 3:
                        combine_exp(t - 1)

            attend(0, False)
            with act.Fori(1, T) as t:
                attend(t, True)
            hidden(T - 1)
            combine_exp(T - 1)

        @block.vector
        def _(dve):
            bank = lambda b, n=1: ps[:, b:b + n, :].rearrange("p b n -> p (b n)")

            for c in range(NQ):
                ts = range(c * TQ, (c + 1) * TQ)
                tt = slice(c * TQ, (c + 1) * TQ)
                n = 20 * c
                dve.wait_ge(x_in[c], 16)
                for t in ts:
                    dve.bn_stats(st[:, t, :], xs[:, t, :]).then_inc(dve_pro, 1)
                dve.wait_ge(dve_pro, n + 4)
                for t in ts:
                    dve.bn_aggr(mv[:, t, :], st[:, t, :]).then_inc(dve_pro, 1)
                dve.wait_ge(dve_pro, n + 8)
                dve.tensor_scalar(mv[:, tt, 1], mv[:, tt, 1], 1e-5, None, ALU.add).then_inc(dve_pro, 4)
                dve.wait_ge(pool_pro, 2 * c + 1)
                for t in ts:
                    dve.tensor_scalar(x1[:, t, :], xs[:, t, :], mv[:, t, 0:1], rstd[:, t:t + 1], ALU.subtract,
                                      ALU.mult).then_inc(xn_ready, 1)
                dve.wait_ge(xn_ready, 4 * (c + 1))
                for t in ts:
                    dve.bn_stats(st2[:, t, :], x1[:, t, :]).then_inc(dve_pro, 1)
                dve.wait_ge(dve_pro, n + 16)
                for t in ts:
                    last = dve.bn_aggr(mv2[:, t, :], st2[:, t, :])
                last.then_inc(dve_pro, 3)
                dve.wait_ge(dve_pro, n + 19)
                dve.tensor_scalar(mv2[:, tt, 1], mv2[:, tt, 1], 1e-3, None, ALU.add).then_inc(dve_pro, 1)
                dve.wait_ge(pool_pro, 2 * c + 2)
                for t in ts:
                    dve.tensor_scalar(xn2[:, t, :], x1[:, t, :], mv2[:, t, 0:1], rstd2[:, t:t + 1],
                                      ALU.subtract, ALU.mult).then_inc(xn2_ready, 1)
                if c == 0:
                    dve.wait_ge(act_pro, 1)
                    dve.wait_ge(wa_in, 16 * NWA)
                    dve.tensor_tensor(wq_s, wq_nat, rowsT[:, 0:CH].unsqueeze(2).broadcast_to([P, CH, C]),
                                      ALU.mult).then_inc(wqk_scaled, 1)
                    dve.wait_ge(wb_in, 16 * NWB)
                    dve.tensor_copy(optT[:].rearrange("p (d h) -> p d h", d=D1),
                                    w_nat[:, 3, :].rearrange("p (h d) -> p d h", d=D1)).then_inc(wqk_scaled, 1)
                    dve.tensor_tensor(wk_s[:], w_kv[:, 0:2, :], rowsT[:, 8:10].unsqueeze(2).broadcast_to([P, 2, C]),
                                      ALU.mult).then_inc(wqk_scaled, 1)
            dve.wait_ge(wb_in, 16 * NWB)
            dve.tensor_reduce(fsc[:, 0:1], tern[:], AX.X, ALU.add, apply_absolute_value=True).then_inc(wabs_ready, 1)
            for c in range(NQ):
                cs = slice(c * QUART, (c + 1) * QUART)
                cp = slice(BLK + c * QUART, BLK + (c + 1) * QUART)
                for k in (0, 1):
                    dve.wait_ge(gx_done, 2 * c + k + 1)
                    if c:
                        dve.wait_ge(ssq_done, c)
                    dve.tensor_tensor(gx[:, k, :], xnT[:, cp], bank(2 + k), ALU.mult).then_inc(gx_ready, 1)
                dve.wait_ge(act_mean, 2 * c + 2)
                for k in (0, 1):
                    dve.reciprocal(gx[:, 2 + k, :], gx[:, 2 + k, :]).then_inc(rms_ready, 1)
                dve.wait_ge(rms_ready, 2 * c + 1)
                dve.tensor_tensor(xqT[:, cs], xnT[:, cp], gx[:, 2, :], ALU.mult).then_inc(xqk_ready, 1)
                dve.wait_ge(rms_ready, 2 * c + 2)
                dve.tensor_tensor(xkT[:, cp], xnT[:, cp], gx[:, 3, :], ALU.mult).then_inc(xqk_ready, 1)
                dve.wait_ge(xf_copied, c + 1)
                dve.tensor_reduce(fsc[:, 1 + c:2 + c], xfT[:, cs], AX.X, ALU.max,
                                  apply_absolute_value=True).then_inc(amax_ready, 1)
            dve.wait_ge(amax_ready, NQ)
            dve.tensor_reduce(fsc[:, 5:6], fsc[:, 1:5], AX.X, ALU.max).then_inc(amax_ready, 1)
            dve.wait_ge(pe_pro, 7)
            dve.tensor_scalar(fsc[:, 10:11], ps[:, 6, 0:1], 1.0 / (C * C), None, ALU.mult).then_inc(tern_step, 1)
            dve.wait_ge(tern_step, 1)
            dve.tensor_scalar(fsc[:, 11:12], fsc[:, 10:11], 1e-5, None, ALU.add).then_inc(tern_step, 1)
            dve.wait_ge(tern_step, 2)
            dve.reciprocal(fsc[:, 12:13], fsc[:, 11:12]).then_inc(tern_step, 1)
            dve.wait_ge(tern_step, 3)
            dve.tensor_scalar(tern[:], tern[:], fsc[:, 12:13], ROUND, ALU.mult, ALU.add).then_inc(tern_step, 1)
            dve.wait_ge(tern_step, 4)
            dve.tensor_scalar(tern[:], tern[:], ROUND, 1.0, ALU.subtract, ALU.min).then_inc(tern_step, 1)
            dve.wait_ge(tern_step, 5)
            dve.tensor_scalar(tern[:], tern[:], -1.0, None, ALU.max).then_inc(tern_step, 1)
            dve.wait_ge(gmax_ready, 1)
            dve.reciprocal(fsc[:, 7:8], fsc[:, 6:7]).then_inc(fsc_ready, 1)
            dve.tensor_scalar(fsc[:, 13:14], fsc[:, 6:7], 1.0 / 128.0, None, ALU.mult).then_inc(fsc_ready, 1)
            dve.wait_ge(fsc_ready, 2)
            dve.tensor_scalar(fsc[:, 8:9], fsc[:, 7:8], 128.0, None, ALU.mult).then_inc(fsc_ready, 1)
            dve.tensor_tensor(fsc[:, 9:10], fsc[:, 13:14], fsc[:, 10:11], ALU.mult).then_inc(fsc_ready, 2)
            dve.wait_ge(fsc_ready, 5)
            dve.wait_ge(bias_in, 16)

            def ffn_input(t, u):
                if later(t, 1):
                    dve.wait_ge(x1_done, t - 1)
                dve.tensor_scalar(ffx[:, u, 0, :], xfT[:, tok(t)], fsc[:, 8:9], LIM, ALU.mult,
                                  ALU.min).then_inc(ffx_step, 1)
                dve.wait_ge(ffx_step, t + 1)
                dve.tensor_scalar(ffx[:, u, 1, :], ffx[:, u, 0, :], -LIM, fsc[:, 9:10], ALU.max,
                                  ALU.mult).then_inc(ffx_ready, 1)

            def add_bias(t, u, h):
                dve.wait_ge(scores_done, t * 2 + h + 1)
                if later(t, 1):
                    dve.wait_ge(pT_done, (t - 1) * 2)
                for r in (0, 1):
                    s = 8 * h + 4 * r
                    bv = biasm[:, 4 * h + 2 * r:4 * h + 2 * r + 2, :].rearrange("p a b -> p (a b)")
                    last = dve.tensor_tensor(sp[:, u, s:s + 4, :].rearrange("p (b a) n -> p b (a n)", b=2),
                                             ps[:, 2 * h + r, :].rearrange("p (b n) -> p b n", b=2),
                                             bv.unsqueeze(1).broadcast_to([P, 2, 2 * P]), ALU.add)
                last.then_inc(bias_added, 1)
                dve.wait_ge(bias_added, t * 2 + h + 1)
                if isinstance(t, int) and t == 0:
                    for r in (0, 1):
                        s = 8 * h + 4 * r
                        last = dve.memset(sp[:, u, s:s + 2, 0:BLK], BIG)
                    last.then_inc(first_masked, 1)

            def row_max(t, u, h):
                if isinstance(t, int) and t == 0:
                    dve.wait_ge(first_masked, h + 1)
                hs = slice(8 * h, 8 * h + 8)
                dve.tensor_reduce(z0[:, u, 0, hs], sp[:, u, hs, :], AX.X, ALU.max,
                                  negate=True).then_inc(nmax_ready, 1)

            def copy_pT(t, h):
                dve.wait_ge(pT_done, t * 2 + h + 1)
                if later(t):
                    dve.wait_ge(y_done, t * 2 + h - 1)
                dve.tensor_copy(pTs[:, h, 4:8, :].rearrange("p a b -> p (a b)"), bank(5)).then_inc(pTd_copied, 1)

            def step(t, u):
                v = 1 - u
                if has(t):
                    dve.wait_ge(kv_done, t + 1)
                    if later(t, 1):
                        dve.wait_ge(scores_done, (t - 1) * 2)
                    dve.tensor_copy(ks[:, u].rearrange("p a b -> p (a b)"), ps[:, 2, 0:2 * WIN]).then_inc(k_copied, 1)
                if has(t, 2):
                    dve.wait_ge(x1_done, t - 1)
                    dve.tensor_tensor(x1[:, bass.ds(t - 2, 1), :].rearrange("p a c -> p (a c)"),
                                      xs[:, bass.ds(t - 2, 1), :].rearrange("p a c -> p (a c)"),
                                      ps[:, 7, 0:C], ALU.add).then_inc(x1_ready, 1)
                    dve.wait_ge(bias_in, 16)
                    dve.wait_ge(x1_ready, t - 1)
                    dve.bn_stats(st3[:, u, :], x1[:, bass.ds(t - 2, 1), :].rearrange("p a c -> p (a c)")).then_inc(st_ready, 1)
                    dve.wait_ge(bias_in, 16)
                    dve.wait_ge(st_ready, t - 1)
                    dve.bn_aggr(mv3[:, u, :], st3[:, u, :]).then_inc(mv_ready, 1)
                    dve.wait_ge(mv_ready, (t - 2) * 2 + 1)
                    dve.tensor_scalar(mv3[:, u, 1:2], mv3[:, u, 1:2], 1e-5, None, ALU.add).then_inc(mv_ready, 1)
                if has(t, 1):
                    copy_pT(t - 1, 0)
                if has(t, 2):
                    dve.wait_ge(rstd_ready, t - 1)
                    if later(t - 2, 1):
                        dve.wait_ge(xT_done, t - 3)
                    dve.tensor_scalar(xn1[:, u, :], x1[:, bass.ds(t - 2, 1), :].rearrange("p a c -> p (a c)"), mv3[:, u, 0:1],
                                      rstd3[:, u:u + 1], ALU.subtract, ALU.mult).then_inc(xn1_ready, 1)
                if has(t):
                    add_bias(t, u, 0)
                    row_max(t, u, 0)
                    add_bias(t, u, 1)
                if has(t, 1):
                    copy_pT(t - 1, 1)
                if has(t):
                    row_max(t, u, 1)
                if has(t, 1):
                    ffn_input(t - 1, v)
                if has(t, 1):
                    dve.wait_ge(y_done, t * 2)
                    if later(t - 1, 1):
                        dve.wait_ge(x1_done, t - 2)
                    dve.tensor_copy(yTs[:, v, 4:8, :].rearrange("p j (b q) -> p b j q", b=2),
                                    ps[:, 6, :].rearrange("p (b j q) -> p b j q", b=2, j=4)).then_inc(yd_copied, 1)
                if has(t, 2):
                    dve.wait_ge(p1_ready, t - 1)
                    if later(t - 2, 1):
                        dve.wait_ge(split_ready, t - 3)
                    dve.tensor_tensor(rem[:, u].rearrange("p a b -> p (a b)"), ps[:, 7, P:3 * P],
                                      parts[:, u, 0].rearrange("p a b -> p (a b)"), ALU.subtract).then_inc(rem_ready, 1)

            tiles(dve, step, 2)

            dve.wait_ge(xn1T_copied, T)
            dve.tensor_reduce(xsum[:, T:T + 1], xsum[:, 0:T], AX.X, ALU.add).then_inc(gate_step, 1)
            dve.wait_ge(gate_pe, 1)
            dve.scalar_tensor_tensor(gate[:, 0, :], ps[0:1, 6, 0:EXPERTS], 1.0 / S, br_s[:], ALU.mult,
                                     ALU.add).then_inc(gate_step, 1)
            dve.wait_ge(gate_step, 2)
            dve.max(gate[:, 1, :], gate[:, 0, :]).then_inc(gate_step, 1)
            dve.wait_ge(gate_step, 3)
            dve.max_index(gidx[:], gate[:, 1, :], gate[:, 0, :]).then_inc(gate_step, 1)

            def row_maxima(t):
                dve.wait_ge(l_max, (t + 1) * NC)
                if later(t):
                    dve.wait_ge(comb, t * 6)
                dve.tensor_reduce(fT[:, 0, 0:H1], lnm[:, bass.ds(t, 1), :].rearrange("p a (h s) -> p (a h) s", s=NS),
                                  AX.X, ALU.min).then_inc(mn_ready, 1)

            def weigh(t):
                dve.wait_ge(f_done, t + 1)
                if later(t):
                    dve.wait_ge(o_done, t)
                dve.tensor_tensor(optT[:], vT[:, tok(t)], ps[:, 6, 0:P], ALU.mult).then_inc(opt_ready, 1)

            def finish(t):
                dve.wait_ge(o_done, t + 1)
                xv = x1[:, bass.ds(t, 1), :].rearrange("p a c -> p (a c)")
                dve.tensor_tensor(xv, xv, ps[:, 7, 0:C], ALU.add).then_inc(o_ready, 1)

            def maxima(t, lagged):
                for k, (h, c, quarters) in enumerate(CHUNKS):
                    dve.wait_ge(l_scores, t * NC + k + 1)
                    i = h * NS + c
                    dve.tensor_reduce(lnm[:, bass.ds(t, 1), i:i + 1].rearrange("p a b -> p (a b)"),
                                      bank(2 * (k % BUFS), len(quarters)), AX.X, ALU.max,
                                      negate=True).then_inc(l_max, 1)
                    if lagged and k == 1:
                        row_maxima(t - 1)
                    if lagged and k == 13:
                        weigh(t - 1)
                    if lagged and k == 19:
                        finish(t - 1)

            dve.wait_ge(chunks_set, 2)
            maxima(0, False)
            with dve.Fori(1, T) as t:
                maxima(t, True)
            row_maxima(T - 1)
            weigh(T - 1)
            finish(T - 1)

        @block.tensor
        def _(pe):
            pe.wait_ge(consts, 9)
            pe.wait_ge(wa_in, 16 * NWA)
            pe.wait_ge(wb_in, 16 * NWB)
            pe.transpose(ps[:, 7, 0:12], rows[:], ident[0:12, 0:12]).then_inc(pe_pro, 1)
            for j in range(CH):
                pe.matmul(ps[:, 6, 0:C], wq_nat[:, j, :], wq_nat[:, j, :], start=(j == 0), stop=(j == CH - 1))
            for j in range(2):
                last = pe.matmul(ps[:, 6, C:2 * C], w_kv[:, j, :], w_kv[:, j, :], start=(j == 0), stop=(j == 1))
            last.then_inc(pe_pro, 1)
            pe.wait_ge(wqk_scaled, 3)
            for j in range(CH):
                last = pe.transpose(ps[:, j // 4, (j % 4) * P:(j % 4 + 1) * P], wq_s[:, j, :], ident[:])
            last.then_inc(pe_pro, 1)
            for j in range(2):
                pe.transpose(ps[:, 2, j * P:(j + 1) * P], wk_s[:, j, :], ident[:])
            for j in range(2, 4):
                last = pe.transpose(ps[:, 2, j * P:(j + 1) * P], w_kv[:, j, :], ident[:])
            last.then_inc(pe_pro, 1)
            for j in range(CH):
                last = pe.transpose(ps[:, 3 + j // 4, (j % 4) * P:(j % 4 + 1) * P], wo_nat[:, j].rearrange("p r d -> p (r d)"), ident[:])
            last.then_inc(pe_pro, 1)
            for j in range(4):
                last = pe.transpose(ps[:, 5, j * P:(j + 1) * P],
                                    w_nat[:, j, :] if j < 3 else optT[:],
                                    ident[:])
            last.then_inc(pe_pro, 1)
            pe.wait_ge(act_pro, 2)
            pe.wait_ge(wabs_ready, 1)
            pe.matmul(ps[:, 6, 0:1], ones[:], fsc[:, 0:1], start=True, stop=True).then_inc(pe_pro, 1)
            pe.wait_ge(act_pro, 6)
            for c in range(NQ):
                ts = range(c * TQ, (c + 1) * TQ)
                pe.wait_ge(xn_ready, 4 * (c + 1))
                for j, t in enumerate(ts):
                    last = pe.transpose(ps[:, c % 2, j * P:(j + 1) * P], x1[:, t, :], ident[:])
                last.then_inc(xnT_done, 1)
                pe.wait_ge(xn2_ready, 4 * (c + 1))
                if c:
                    pe.wait_ge(xf_copied, c)
                for j, t in enumerate(ts):
                    last = pe.transpose(ps[:, 7, j * P:(j + 1) * P], xn2[:, t, :], ident[:])
                last.then_inc(xfT_done, 1)
                pe.wait_ge(xn_copied, c + 1)
                if c:
                    pe.wait_ge(gx_ready, 2 * c)
                cp = slice(BLK + c * QUART, BLK + (c + 1) * QUART)
                for k in (0, 1):
                    pe.matmul(ps[:, 2 + k, :], gram[:, k, :], xnT[:, cp], start=True, stop=True).then_inc(gx_done, 1)
                pe.wait_ge(gx_ready, 2 * (c + 1))
                if c:
                    pe.wait_ge(act_mean, 2 * c)
                for k in (0, 1):
                    last = pe.matmul(ps[:, 4 + k, :], ones[:], gx[:, k, :], start=True, stop=True)
                last.then_inc(ssq_done, 1)

            def project(t, u):
                pe.wait_ge(win_ready, t + 1)
                if later(t):
                    pe.wait_ge(bias_added, t * 2)
                qv = ps[:, 0:2, :].rearrange("p c (g b a q) -> p c g a b q", g=2, b=2, a=2)
                for j in range(CH):
                    last = pe.matmul(qv[:, j // 4, j % 4 // 2, j % 2], wqT[:, j, :], xqT[:, tok(t)],
                                     start=True, stop=True)
                last.then_inc(q_done, 1)
                for j in range(2):
                    pe.matmul(ps[:, 2, j * WIN:(j + 1) * WIN], wkvT[:, j, :], xkT[:, bass.ds(t * P, WIN)],
                              start=True, stop=True)
                for b in range(2):
                    last = pe.matmul(ps[:, 3, b * 2 * C:(b + 1) * 2 * C], win[:, u, b * BLK:b * BLK + P],
                                     wkvT[:, 2:4, :].rearrange("p a b -> p (a b)"), start=True, stop=True)
                last.then_inc(kv_done, 1)

            def scores(t, u, h):
                pe.wait_ge(q_copied, t + 1)
                pe.wait_ge(k_copied, t + 1)
                if h:
                    pe.wait_ge(v_copied, t + 1)
                for b in range(2):
                    for a in range(2):
                        for r in range(2):
                            rr = slice(r * HD, (r + 1) * HD)
                            last = pe.matmul(ps[:, 2 * h + r, (2 * b + a) * P:(2 * b + a + 1) * P],
                                             qs[rr, u, 4 * h + 2 * a + b, :],
                                             ks[rr, u, h, b * BLK:b * BLK + P], start=True, stop=True)
                last.then_inc(scores_done, 1)

            def transpose_probs(t, u, h):
                pe.wait_ge(probs_ready, t * 2 + h + 1)
                if later(t) or h:
                    pe.wait_ge(pTa_copied, t * 2 + h)
                    pe.wait_ge(pTd_copied, t * 2 + h)
                for s in range(8):
                    last = pe.transpose(ps[:, 4 + s // 4, (s % 4) * P:(s % 4 + 1) * P], sp[:, u, 8 * h + s, :], ident[:])
                last.then_inc(pT_done, 1)

            def values(t, u, h):
                pe.wait_ge(pTa_copied, t * 2 + h + 1)
                pe.wait_ge(pTd_copied, t * 2 + h + 1)
                if h:
                    pe.wait_ge(ya_copied, t + 1)
                elif later(t):
                    pe.wait_ge(yd_copied, t)
                else:
                    pe.wait_ge(tern_step, 1)
                for b in range(2):
                    for r in range(2):
                        g = 2 * h + r
                        last = pe.matmul(ps[r * HD:(r + 1) * HD, 6, b * 256:(b + 1) * 256],
                                         vs[:, u, b, g * HD:(g + 1) * HD],
                                         pTs[:, h, 4 * r + 2 * b:4 * r + 2 * b + 2, :].rearrange("p a b -> p (a b)"),
                                         start=True, stop=True)
                last.then_inc(y_done, 1)

            def project_out(t, u):
                pe.wait_ge(ya_copied, t + 1)
                pe.wait_ge(yd_copied, t + 1)
                pe.wait_ge(ffx_ready, t + 1)
                if later(t):
                    pe.wait_ge(rem_ready, t)
                elif isinstance(t, int):
                    pe.wait_ge(tern_step, 6)
                for j in range(CH):
                    pe.matmul(ps[:, 7, 0:C], yTs[:, u, j, :], woT[:, j, :], start=(j == 0), stop=False)
                pe.matmul(ps[:, 7, 0:C], ffx[:, u, 1, :], tern[:], start=False, stop=True).then_inc(x1_done, 1)

            def step(t, u):
                v = 1 - u
                if has(t):
                    if isinstance(t, int) and t == 0:
                        pe.wait_ge(xqk_ready, 2 * NQ)
                        pe.wait_ge(act_pro, 7)
                        pe.wait_ge(act_mean, 2 * NQ)
                        pe.wait_ge(xf_copied, NQ)
                    project(t, u)
                if has(t, 2):
                    project_out(t - 2, u)
                if has(t, 1):
                    transpose_probs(t - 1, v, 0)
                if has(t):
                    scores(t, u, 0)
                    scores(t, u, 1)
                if has(t, 2):
                    pe.wait_ge(xn1_ready, t - 1)
                    pe.transpose(ps[:, 7, 0:P], xn1[:, u, :], ident[:]).then_inc(xT_done, 1)
                if has(t, 1):
                    values(t - 1, v, 0)
                    transpose_probs(t - 1, v, 1)
                if has(t, 2):
                    pe.wait_ge(xn1T_copied, t - 1)
                    for s in range(3):
                        o = ps[:, 7, (s + 1) * P:(s + 2) * P]
                        pe.matmul(o, w_inT[:, s].rearrange("p d h -> p (d h)"), xn1T[:, tok(t - 2)],
                                  start=True, stop=False)
                        last = pe.matmul(o, bin_row[:, s].rearrange("p d h -> p (d h)"), ones[0:1, :],
                                         start=False, stop=True)
                    last.then_inc(qkv_done, 1)
                if has(t, 1):
                    values(t - 1, v, 1)

            tiles(pe, step, 2)

            pe.wait_ge(gate_step, 1)
            pe.matmul(ps[0:1, 6, 0:EXPERTS], xsum[:, T:T + 1], wr_s[:], start=True, stop=True).then_inc(gate_pe, 1)

            def replicate(t):
                pe.wait_ge(comb, t * 6 + 6)
                pe.wait_ge(h_ready, t + 1)
                pe.matmul(ps[:, 6, 0:P], frep[:],
                          ident[:], start=True, stop=True).then_inc(f_done, 1)

            def result(t, n):
                o = ps[:, 7, 0:C]
                if n == 0:
                    if later(t):
                        pe.wait_ge(o_ready, t)
                    pe.matmul(o, ones[0:2, :], outb[:], start=True, stop=False)
                elif n <= FC:
                    if n == 1:
                        pe.wait_ge(h_ready, t + 1)
                    pe.matmul(o, hT[:, n - 1, :], w2e[:, n - 1, :], start=False, stop=False)
                else:
                    pe.wait_ge(opt_ready, t + 1)
                    pe.matmul(o, optT[:], w_outT[:], start=False, stop=True).then_inc(o_done, 1)

            def hidden(t, n):
                f = n // 2
                o = ps[:, 6, f * P:(f + 1) * P]
                if n == 0:
                    if later(t):
                        pe.wait_ge(opt_ready, t)
                    else:
                        pe.wait_ge(exp_in, 64)
                        pe.wait_ge(gate_step, 2)
                if n % 2 == 0:
                    pe.matmul(o, w1e[:, f * P:(f + 1) * P], xn1T[:, tok(t)], start=True, stop=False)
                else:
                    last = pe.matmul(o, c1row[:, f * P:(f + 1) * P], ones[0:1, :], start=False, stop=True)
                    if n == 2 * FC - 1:
                        last.then_inc(h_done, 1)

            def attend(t, first, lagged):
                for k, (h, c, quarters) in enumerate(CHUNKS):
                    b = 2 * (k % BUFS)
                    if not first or k >= BUFS:
                        pe.wait_ge(l_slots, t * NC + (k + 1 - BUFS))
                    if h % 8 == 0 and c == 0:
                        pe.wait_ge(q_in[h // 8], (t + 1) * 16)
                    if first and k == 0:
                        pe.wait_ge(kst_in[0], 16 * 3 * (NQ - 1))
                    if first and k == 1:
                        pe.wait_ge(kst_in[3], 48)
                    for n, q in enumerate(quarters):
                        rhs = kst[:, q, h, :] if q < 3 else kst3[0:ROWS, h, :]
                        last = pe.matmul(ps[:, b + n, :], qst[0:ROWS, h, :], rhs, start=True, stop=True)
                    last.then_inc(l_scores, 1)
                    if k % 2 == 0:
                        continue
                    if lagged and k == 1:
                        result(t - 1, 0)
                    if lagged and k == 11:
                        replicate(t - 1)
                    if lagged and k in (3, 5, 7, 9):
                        result(t - 1, (k - 1) // 2)
                    if lagged and k == 15:
                        result(t - 1, 5)
                    if k >= 17:
                        hidden(t, (k - 17) // 2)

            pe.wait_ge(rem_ready, T)
            pe.wait_ge(exp_done, 2 * T)
            pe.wait_ge(bias_added, 2 * T)
            pe.wait_ge(pTa_copied, 2 * T)
            pe.wait_ge(pTd_copied, 2 * T)
            attend(0, True, False)
            with pe.Fori(1, T) as t:
                attend(t, False, True)
            for n in range(5):
                result(T - 1, n)
            replicate(T - 1)
            result(T - 1, 5)


_INS = ["L0_attn_x", "L0_attn_wq", "L0_attn_wk", "L0_attn_wv", "L0_attn_wo", "L0_attn_q_norm_w", "L0_attn_k_norm_w",
        "L0_ffn_weight", "L0_ffn_ln_gamma", "L0_ffn_ln_beta", "L1_attn_w_in", "L1_attn_b_in", "L1_attn_w_out",
        "L1_attn_b_out", "L1_ffn_Wr", "L1_ffn_br", "L1_ffn_W1", "L1_ffn_b1", "L1_ffn_W2", "L1_ffn_b2"]


def alibi_table():
    import numpy as _np
    slopes = _np.array([(2.0 ** (-8.0 / HEADS)) ** (i + 1) for i in range(HEADS)], dtype=_np.float32)
    rel = _np.arange(P)[None, :] - BLK - _np.arange(BLK)[:, None]
    seen = (rel <= 0) & (rel >= -BLK)
    tab = _np.zeros((2, BLK, 8, P), _np.float32)
    for a in range(2):
        for s in range(8):
            cph, r, cpl = s // 4, s // 2 % 2, s % 2
            tab[a, :, s, :] = _np.where(seen, slopes[head_of(cph, r, 2 * cpl + a)] * rel.astype(_np.float32), BIG)
    return tab.reshape(P, 8, P)


def kernel(**inputs):
    import numpy as _np
    import concourse.bacc as _bacc
    from concourse import mybir as _mybir
    from concourse.bass_utils import run_bass_kernel_spmd as _run

    nc = _bacc.Bacc("TRN2", target_bir_lowering=False, num_devices=1)
    arrays, args = {}, []
    named = [(n, _np.ascontiguousarray(inputs[n])) for n in _INS] + [("alibi", alibi_table())]
    for name, a in named:
        arrays[f"in_{name}"] = a
        args.append(nc.dram_tensor(f"in_{name}", a.shape, _mybir.dt.from_np(a.dtype), kind="ExternalInput").ap())
    shape = inputs["L0_attn_x"].shape
    args.append(nc.dram_tensor("out_0", shape, _mybir.dt.float32, kind="ExternalOutput").ap())
    two_layers(nc, *args)
    r = _run(nc, [arrays], core_ids=[0])
    return r.results[0]["out_0"]
```

```python
from contextlib import ExitStack

import concourse.bass as bass
from concourse import mybir

F32 = mybir.dt.float32
BF16 = mybir.dt.bfloat16
U32 = mybir.dt.uint32
ALU = mybir.AluOpType
ACT = mybir.ActivationFunctionType
AX = mybir.AxisListType
RMAX = bass.bass_isa.ReduceOp.max

P = 128
C = 128
HEADS, KV, HD = 16, 4, 64
BLK = 64
WIN = P + BLK
CH = HEADS * HD // P
H1, D1 = 16, 8
PAIRS = ((0, 0), (0, 1), (0, 2), (1, 0), (1, 1), (2, 0))
ROWS = len(PAIRS) * D1
QUART = 512
NS, BUFS = 2, 4
OTHERS = {10: "A", 16: "B", 22: "C", 28: "D"}
HALVES = [(h, s) for h in range(H1) for s in range(NS)]
NC = len(HALVES)
TURNS = list(HALVES)
for _p in sorted(OTHERS):
    TURNS.insert(_p, OTHERS[_p])
AT = {v: k for k, v in OTHERS.items()}
EXPERTS, FF = 8, 512
FC = FF // P
BIG = -1e30
ROUND = 1.5 * 2.0 ** 23
LIM = 128.0 - 1e-5


def head_of(cph, r, j):
    return cph * 8 + r * 4 + j


def two_layers(nc, x, wq, wk, wv, wo, q_norm_w, k_norm_w, ffn_w, ln_gamma, ln_beta,
               w_in, b_in, w_out, b_out, Wr, br, W1, b1, W2, b2, alibi, out):
    _, S, _ = x.shape
    T = S // P
    NQ = S // QUART
    TQ = QUART // P

    with ExitStack() as ctx:
        def sb(name, shape, dt=F32):
            return ctx.enter_context(nc.sbuf_tensor(name, shape, dt))

        def sem(name):
            return ctx.enter_context(nc.semaphore(name))

        ps = ctx.enter_context(nc.psum_tensor("ps", [P, 8, 512], F32))

        ident = sb("ident", [P, P])
        ones = sb("ones", [P, P])
        cst = sb("cst", [P, 8])
        rows = sb("rows", [12, P])
        rowsT = sb("rowsT", [P, 12])
        w_kv = sb("w_kv", [P, 4, C])
        wk_s = sb("wk_s", [P, 2, C])
        gram = sb("gram", [P, 2, C])
        wqT = sb("wqT", [C, CH, P])
        wkvT = sb("wkvT", [C, 4, P])
        woT = sb("woT", [P, CH, C])
        tern = sb("tern", [C, C])
        w_inT = sb("w_inT", [C, 3, D1, H1])
        w_outT = sb("w_outT", [P, C])
        bin_nat = sb("bin_nat", [1, 3 * C])
        bin_row = sb("bin_row", [1, 3, D1, H1])
        outb = sb("outb", [P, 3, C])
        c1T = sb("c1T", [P, FC])
        wr_s = sb("wr_s", [C, EXPERTS])
        br_s = sb("br_s", [1, EXPERTS])
        gate = sb("gate", [1, 3, EXPERTS])
        gidx = sb("gidx", [1, EXPERTS], U32)
        xsum = sb("xsum", [C, T + 1])
        st = sb("st", [P, T, 6])
        mv = sb("mv", [P, T, 2])
        rstd = sb("rstd", [P, T])
        st2 = sb("st2", [P, T, 6])
        mv2 = sb("mv2", [P, T, 2])
        rstd2 = sb("rstd2", [P, T])
        st3 = sb("st3", [P, 2, 6])
        mv3 = sb("mv3", [P, 2, 2])
        rstd3 = sb("rstd3", [P, 2])
        fsc = sb("fsc", [P, 16])
        xs = sb("xs", [P, T, C])
        x1 = sb("x1", [P, T, C])
        xnT = sb("xnT", [C, BLK + S])
        xkT = sb("xkT", [C, BLK + S])
        xqf = sb("xqf", [C, 2, S])
        xqT, xfT = xqf[:, 0, :], xqf[:, 1, :]
        biasm = sb("biasm", [P, 8, P])
        qs = sb("qs", [P, 2, CH, P])
        ks = sb("ks", [P, 2, 2, WIN])
        vs = sb("vs", [P, 2, 2, 2 * C])
        win = sb("win", [C, 2, WIN])
        ffx = sb("ffx", [C, 2, 2, P])
        sp = sb("sp", [P, 2, 16, P])
        z0 = sb("z0", [P, 2, 3, 16])
        pTs = sb("pTs", [P, 2, 8, P])
        yTs = sb("yTs", [P, 2, CH, P])
        xn1 = sb("xn1", [P, 2, C])
        xn1T = sb("xn1T", [C, S])
        vT = sb("vT", [P, S])
        rem = sb("rem", [P, 2, 2, P])
        parts = sb("parts", [P, 2, 3, 2, P], BF16)
        kst = sb("kst", [ROWS, 3, H1, QUART], BF16)
        fT = sb("fT", [P, 6, NS * H1])
        frep = sb("frep", [P, P])
        lnm = sb("lnm", [P, T, NS * H1])
        lz = sb("lz", [P, T, NS * H1])
        optT = sb("optT", [P, P])

        wq_nat = pTs[:].rearrange("p a b c -> p (a b) c")[:, 0:CH, :]
        wq_s = pTs[:].rearrange("p a b c -> p (a b) c")[:, CH:2 * CH, :]
        wo_nat = yTs[:, 0].rearrange("p a (r d) -> p a r d", r=2)
        w_nat = xn1T[:, 0:4 * C].rearrange("p (a c) -> p a c", a=4)
        xn2 = sp[:, 0]
        gx = sp[:, 1].rearrange("p a b -> p (a b)").rearrange("p (k n) -> p k n", k=4)
        kst3 = xqf[:].rearrange("p a b -> p (a b)").bitcast(BF16).rearrange("p (h n) -> p h n", h=H1)
        qst = xnT[:, 0:S].bitcast(BF16).rearrange("p (h n) -> p h n", n=P)[:, 0:H1, :]
        w1e = xkT[:, 0:FF]
        w2e = xkT[:, FF:2 * FF].rearrange("p (f c) -> p f c", f=FC)
        hT = xkT[:, 2 * FF:3 * FF].rearrange("p (f c) -> p f c", f=FC)

        scr_k = nc.dram_tensor("scr_k", [3, P, S], BF16, kind="Internal").ap()
        scr_q = nc.dram_tensor("scr_q", [len(PAIRS), P, S], BF16, kind="Internal").ap()

        x_in = [sem(f"x_in{c}") for c in range(NQ)]
        wa_in, wb_in, bias_in = sem("wa_in"), sem("wb_in"), sem("bias_in")
        consts = sem("consts")
        dve_pro, pool_pro, act_pro, pe_pro = sem("dve_pro"), sem("pool_pro"), sem("act_pro"), sem("pe_pro")
        xn_ready, xn2_ready, xnT_done, xn_copied, xfT_done, xf_copied = (
            sem("xn_ready"), sem("xn2_ready"), sem("xnT_done"), sem("xn_copied"), sem("xfT_done"), sem("xf_copied"))
        gx_done, gx_ready, ssq_done, act_mean, rms_ready, xqk_ready = (
            sem("gx_done"), sem("gx_ready"), sem("ssq_done"), sem("act_mean"), sem("rms_ready"), sem("xqk_ready"))
        amax_ready, gmax_ready, fsc_ready, wabs_ready, tern_step, wqk_scaled, first_masked = (
            sem("amax_ready"), sem("gmax_ready"), sem("fsc_ready"), sem("wabs_ready"), sem("tern_step"),
            sem("wqk_scaled"), sem("first_masked"))
        win_ready, ffx_ready = sem("win_ready"), sem("ffx_ready")
        q_done, kv_done = sem("q_done"), sem("kv_done")
        q_copied, v_copied, k_copied = sem("q_copied"), sem("v_copied"), sem("k_copied")
        scores_done, bias_added, nmax_ready, exp_done = (
            sem("scores_done"), sem("bias_added"), sem("nmax_ready"), sem("exp_done"))
        rz_ready, probs_ready = sem("rz_ready"), sem("probs_ready")
        pT_done, pTa_copied, pTd_copied = sem("pT_done"), sem("pTa_copied"), sem("pTd_copied")
        y_done, ya_copied, yd_copied = sem("y_done"), sem("ya_copied"), sem("yd_copied")
        x1_done, x1_ready, st_ready, mv_ready, rstd_ready, xn1_ready = (
            sem("x1_done"), sem("x1_ready"), sem("st_ready"), sem("mv_ready"), sem("rstd_ready"), sem("xn1_ready"))
        xT_done, xn1T_copied, qkv_done = sem("xT_done"), sem("xn1T_copied"), sem("qkv_done")
        p1_ready, rem_ready, p2_ready, split_ready = (
            sem("p1_ready"), sem("rem_ready"), sem("p2_ready"), sem("split_ready"))
        scr_w = [sem("scr_w0"), sem("scr_w1")]
        kst_in = [sem(f"kst_in{q}") for q in range(NQ)]
        ffx_step = sem("ffx_step")
        gate_step, gate_pe, exp_in = sem("gate_step"), sem("gate_pe"), sem("exp_in")
        q_in = [sem("q_in0"), sem("q_in1")]
        l_scores, l_max, l_slots = sem("l_scores"), sem("l_max"), sem("l_slots")
        mn_ready, h_ready = sem("mn_ready"), sem("h_ready")
        biased, ffn_done, ffn_added = sem("biased"), sem("ffn_done"), sem("ffn_added")
        h_done, comb, comb_e, f_done, opt_ready, o_done, o_ready, stored = (
            sem("h_done"), sem("comb"), sem("comb_e"), sem("f_done"), sem("opt_ready"), sem("o_done"),
            sem("o_ready"), sem("stored"))

        block = ctx.enter_context(nc.Block())

        def tiles(eng, step, lag):
            for t in range(4):
                step(t, t % 2)
            with eng.Fori(2, T // 2) as i:
                for u in (0, 1):
                    step(i * 2 + u, u)
            for t in range(T, T + lag):
                step(t, t % 2)

        def has(t, lag=0):
            return not isinstance(t, int) or 0 <= t - lag < T

        def later(t, n=0):
            return not isinstance(t, int) or t - n > 0

        def tok(t):
            return bass.ds(t * P, P)

        NWA, NWB = 11, 13

        @block.sync
        def _(sp_):
            xv = x.rearrange("a (c t p) d -> (a c) p t d", c=NQ, p=P)
            for c in range(NQ):
                sp_.dma_start(xs[:, c * TQ:(c + 1) * TQ, :], xv[c]).then_inc(x_in[c], 16)
            sp_.dma_start(biasm[:], alibi).then_inc(bias_in, 16)

            def write_parts(t, u):
                sp_.wait_ge(split_ready, t + 1)
                sp_.dma_start(scr_k[:, :, tok(t)].rearrange("j p n -> p j n"),
                              parts[:, u, :, 1, :]).then_inc(scr_w[u], 16)
                for i, (a, n) in enumerate(((0, 3), (3, 2), (5, 1))):
                    sp_.dma_start(scr_q[a:a + n, :, tok(t)].rearrange("j p n -> p j n"),
                                  parts[:, u, i:i + 1, 0, :].broadcast_to([P, n, P])).then_inc(scr_w[u], 16)

            def read_keys(q, dst, signal):
                for u in (0, 1):
                    sp_.wait_ge(scr_w[u], (q * (TQ // 2) + TQ // 2) * 64)
                src = scr_k.rearrange("j (d h) n -> (j d) h n", h=H1)
                for a, n in ((0, 3), (3, 2), (5, 1)):
                    sp_.dma_start(dst[a * D1:(a + n) * D1], src[0:n * D1, :, bass.ds(q * QUART, QUART)]
                                  ).then_inc(signal, 16)

            with sp_.Fori(0, NQ - 1) as q:
                for j in range(TQ):
                    write_parts(q * TQ + j, j % 2)
                read_keys(q, kst[:, bass.ds(q, 1)].rearrange("p a h n -> p (a h) n"), kst_in[0])
            for j in range(TQ):
                write_parts((NQ - 1) * TQ + j, j % 2)
            sp_.wait_ge(q_done, T)
            sp_.wait_ge(ffx_ready, T)
            read_keys(NQ - 1, kst3[0:ROWS], kst_in[3])

            qsrc = scr_q.rearrange("j (d h) n -> (j d) h n", h=H1)
            sp_.wait_ge(win_ready, T)

            def read_q(t, g):
                hs = slice(g * 8, g * 8 + 8)
                sp_.dma_start(qst[0:ROWS, hs, :], qsrc[:, hs, tok(t)]).then_inc(q_in[g], 16)

            read_q(0, 0)
            read_q(0, 1)
            sp_.wait_ge(kv_done, T)
            sp_.wait_ge(gate_step, 4)
            e = sp_.value_load(gidx[0:1, 0:1], min_val=0, max_val=EXPERTS - 1)
            sp_.dma_start(w1e, W1[bass.ds(e, 1)].rearrange("e c f -> (e c) f")).then_inc(exp_in, 16)
            sp_.dma_start(c1T[:], b1[bass.ds(e, 1), :].rearrange("e (p f) -> p (e f)", f=FC)).then_inc(exp_in, 16)
            sp_.dma_start(w2e, W2[bass.ds(e, 1)].rearrange("e (p f) c -> p (e f) c", f=FC)).then_inc(exp_in, 16)
            sp_.dma_start(outb[:, 1, :], b2[bass.ds(e, 1), :].broadcast_to([P, C])).then_inc(exp_in, 16)
            ov = out.rearrange("a (t p) d -> (a t) p d", p=P)
            with sp_.Fori(1, T) as t:
                sp_.wait_ge(l_scores, t * NC - (NC - 16))
                read_q(t, 0)
                sp_.wait_ge(l_scores, t * NC)
                read_q(t, 1)
                sp_.wait_ge(o_ready, t)
                sp_.dma_start(ov[bass.ds(t - 1, 1)].rearrange("a p d -> p (a d)"),
                              x1[:, bass.ds(t - 1, 1), :].rearrange("p a d -> p (a d)")).then_inc(stored, 16)
            sp_.wait_ge(o_ready, T)
            sp_.dma_start(ov[T - 1], x1[:, T - 1, :]).then_inc(stored, 16)
            sp_.wait_ge(stored, 16 * T)

        @block.gpsimd
        def _(pool):
            pool.memset(ident[:], 0.0).then_inc(consts, 1)
            pool.memset(ones[:], 1.0).then_inc(consts, 1)
            pool.memset(cst[:, 0:1], -0.5).then_inc(consts, 1)
            pool.memset(cst[:, 1:2], -1.0).then_inc(consts, 1)
            pool.memset(cst[:, 2:3], 1e-6).then_inc(consts, 1)
            pool.memset(cst[:, 3:4], 0.0).then_inc(consts, 1)
            pool.wait_ge(consts, 6)
            pool.affine_select(out=ident[:], in_=ident[:], compare_op=ALU.not_equal, fill=1.0, base=0,
                               pattern=[[-1, P]], channel_multiplier=1).then_inc(consts, 1)
            pool.memset(xnT[:, 0:BLK], 0.0).then_inc(consts, 1)
            pool.memset(xkT[:, 0:BLK], 0.0).then_inc(consts, 1)
            pool.wait_ge(consts, 9)

            def power(o, i, col, n):
                return pool.tensor_tensor(o, i, cst[:, col:col + 1].broadcast_to([P, n]), ALU.pow)

            for c in range(NQ):
                ts = slice(c * TQ, (c + 1) * TQ)
                pool.wait_ge(dve_pro, 20 * c + 12)
                power(rstd[:, ts], mv[:, ts, 1], 0, TQ).then_inc(pool_pro, 1)
                pool.wait_ge(dve_pro, 20 * c + 20)
                power(rstd2[:, ts], mv2[:, ts, 1], 0, TQ).then_inc(pool_pro, 1)
            pool.wait_ge(amax_ready, NQ + 1)
            pool.partition_all_reduce(fsc[:, 6:7], fsc[:, 5:6], P, RMAX).then_inc(gmax_ready, 1)

            def window(t, u):
                if later(t, 1):
                    pool.wait_ge(kv_done, t - 1)
                pool.tensor_tensor(win[:, u, :], xnT[:, bass.ds(t * P, WIN)], cst[:, 3:4].broadcast_to([P, WIN]),
                                   ALU.add).then_inc(win_ready, 1)

            pool.wait_ge(xn_copied, NQ)
            window(0, 0)

            def step(t, u):
                v = 1 - u
                if has(t, -1) and (not isinstance(t, int) or t + 1 < T):
                    window(t + 1, v)
                if has(t, 2):
                    pool.wait_ge(mv_ready, (t - 1) * 2)
                    power(rstd3[:, u:u + 1], mv3[:, u, 1:2], 0, 1).then_inc(rstd_ready, 1)

                def normalize(h):
                    hs = slice(8 * h, 8 * h + 8)
                    pool.wait_ge(exp_done, t * 2 + h + 1)
                    power(z0[:, u, 2, hs], z0[:, u, 1, hs], 1, 8).then_inc(rz_ready, 1)
                    pool.wait_ge(rz_ready, t * 2 + h + 1)
                    pool.tensor_tensor(sp[:, u, hs, :], sp[:, u, hs, :],
                                       z0[:, u, 2, hs].unsqueeze(2).broadcast_to([P, 8, P]),
                                       ALU.mult).then_inc(probs_ready, 1)

                if has(t):
                    normalize(0)
                if has(t, 2):
                    pool.wait_ge(rem_ready, t - 1)
                    pool.tensor_tensor(parts[:, u, 1], rem[:, u], cst[:, 3:4].unsqueeze(2).broadcast_to([P, 2, P]),
                                       ALU.add).then_inc(p2_ready, 1)
                    pool.wait_ge(p2_ready, t - 1)
                    pool.tensor_tensor(parts[:, u, 2], rem[:, u], parts[:, u, 1],
                                       ALU.subtract).then_inc(split_ready, 1)
                if has(t):
                    normalize(1)

            for t in range(4):
                step(t, t % 2)
            with pool.Fori(2, T // 2 - 1) as i:
                for u in (0, 1):
                    step(i * 2 + u, u)
            for t in range(T - 2, T + 2):
                step(t, t % 2)

            def combine(t):
                m = lnm[:, bass.ds(t, 1), :].rearrange("p a (h s) -> p (a h) s", s=NS)
                z = lz[:, bass.ds(t, 1), :].rearrange("p a (h s) -> p (a h) s", s=NS)
                d, e, w = (fT[:, k, :].rearrange("p (h s) -> p h s", s=NS) for k in range(1, 4))
                n = t * 5
                pool.wait_ge(l_slots, (t + 1) * NC)
                pool.wait_ge(mn_ready, t + 1)
                pool.tensor_tensor(d, fT[:, 0, 0:H1].unsqueeze(2).broadcast_to([P, H1, NS]), m,
                                   ALU.subtract).then_inc(comb, 1)
                pool.wait_ge(comb_e, t + 1)
                pool.tensor_tensor(w, z, e, ALU.mult).then_inc(comb, 1)
                pool.wait_ge(comb, n + 2)
                pool.tensor_tensor(fT[:, 4, 0:H1], w[:, :, 0], w[:, :, 1], ALU.add).then_inc(comb, 1)
                pool.wait_ge(comb, n + 3)
                power(fT[:, 5, 0:H1], fT[:, 4, 0:H1], 1, H1).then_inc(comb, 1)
                pool.wait_ge(comb, n + 4)
                pool.tensor_tensor(frep[:].rearrange("p (d h) -> p d h", d=D1),
                                   fT[:, 4:5, 0:H1].broadcast_to([P, D1, H1]),
                                   fT[:, 5:6, 0:H1].broadcast_to([P, D1, H1]), ALU.mult).then_inc(comb, 1)

            pool.wait_ge(exp_in, 64)
            pool.tensor_tensor(outb[:, 2, :], outb[:, 0, :], outb[:, 1, :], ALU.add).then_inc(biased, 1)
            pool.wait_ge(biased, 1)
            pool.tensor_tensor(x1[:], x1[:], outb[:, 2:3, :].broadcast_to([P, T, C]), ALU.add).then_inc(biased, 1)

            with pool.Fori(0, T) as t:
                combine(t)

        @block.scalar
        def _(act):
            r_of = lambda r: slice(r * HD, (r + 1) * HD)
            wqv = wq.rearrange("(cph r j d) c -> r d cph j c", cph=2, r=2, j=4)
            wov = wo.rearrange("o (cph r j d) -> o cph r j d", cph=2, r=2, j=4)
            qnv = q_norm_w.rearrange("(cph r j d) -> cph r j d", cph=2, r=2, j=4)
            for cph in (0, 1):
                for r in (0, 1):
                    act.dma_start(wq_nat[r_of(r), cph * 4:cph * 4 + 4, :], wqv[r, :, cph]).then_inc(wa_in, 16)
            act.dma_start(w_kv[:, 0:2, :], wk.rearrange("(a p) c -> p a c", p=P)).then_inc(wa_in, 16)
            act.dma_start(w_kv[:, 2:4, :], wv.rearrange("(a p) c -> p a c", p=P)).then_inc(wa_in, 16)
            for cph in (0, 1):
                for r in (0, 1):
                    act.dma_start(rows[cph * 4:cph * 4 + 4, r_of(r)], qnv[cph, r]).then_inc(wa_in, 16)
            act.dma_start(rows[8:10, :], k_norm_w.rearrange("(a p) -> a p", p=P)).then_inc(wa_in, 16)
            act.dma_start(rows[10:11, :], ln_gamma.unsqueeze(0)).then_inc(wb_in, 16)
            act.dma_start(rows[11:12, :], ln_beta.unsqueeze(0)).then_inc(wb_in, 16)
            for cph in (0, 1):
                for r in (0, 1):
                    act.dma_start(wo_nat[:, cph * 4:cph * 4 + 4, r, :], wov[:, cph, r]).then_inc(wb_in, 16)
            act.dma_start(tern[:], ffn_w).then_inc(wb_in, 16)
            act.dma_start(w_nat[:, 0:3, :], w_in.rearrange("(a p) c -> p a c", p=P)).then_inc(wb_in, 16)
            act.dma_start(w_nat[:, 3, :], w_out).then_inc(wb_in, 16)
            act.dma_start(bin_nat[:], b_in.unsqueeze(0)).then_inc(wb_in, 16)
            act.dma_start(outb[:, 0, :], b_out.unsqueeze(0).broadcast_to([P, C])).then_inc(wb_in, 16)
            act.dma_start(wr_s[:], Wr).then_inc(wb_in, 16)
            act.dma_start(br_s[:], br.unsqueeze(0)).then_inc(wb_in, 16)

            def copy(o, i, signal, **kw):
                return act.activation(o, i, ACT.Identity, **kw).then_inc(signal, 1)

            bank = lambda b, n=1: ps[:, b:b + n, :].rearrange("p b n -> p (b n)")
            act.wait_ge(pe_pro, 1)
            copy(rowsT[:], ps[:, 7, 0:12], act_pro)
            act.wait_ge(pe_pro, 2)
            copy(gram[:], ps[:, 6, 0:2 * C].rearrange("p (a c) -> p a c", a=2), act_pro)
            act.wait_ge(pe_pro, 3)
            copy(wqT[:].rearrange("p a b -> p (a b)"), bank(0, 2), act_pro, scale=HD ** -0.5)
            act.wait_ge(pe_pro, 4)
            copy(wkvT[:].rearrange("p a b -> p (a b)"), bank(2), act_pro)
            act.wait_ge(pe_pro, 5)
            copy(woT[:].rearrange("p a b -> p (a b)"), bank(3, 2), act_pro)
            act.wait_ge(pe_pro, 6)
            win_v = ps[:, 5, 0:3 * C].rearrange("p (h s d) -> p s d h", s=3, d=D1)
            act.activation(w_inT[:, 0], win_v[:, 0], ACT.Identity, scale=D1 ** -0.5)
            act.activation(w_inT[:, 1], win_v[:, 1], ACT.Identity)
            act.activation(w_inT[:, 2], win_v[:, 2], ACT.Identity)
            copy(w_outT[:], ps[:, 5, 3 * C:4 * C], act_pro)
            bin_v = bin_nat[:].rearrange("p (h s d) -> p s d h", s=3, d=D1)
            act.activation(bin_row[:, 0], bin_v[:, 0], ACT.Identity, scale=D1 ** -0.5)
            act.activation(bin_row[:, 1], bin_v[:, 1], ACT.Identity)
            copy(bin_row[:, 2], bin_v[:, 2], act_pro)
            for c in range(NQ):
                act.wait_ge(xnT_done, c + 1)
                copy(xnT[:, BLK + c * QUART:BLK + (c + 1) * QUART], bank(c % 2), xn_copied)
                act.wait_ge(xfT_done, c + 1)
                if c == 0:
                    act.wait_ge(act_pro, 1)
                copy(xfT[:, c * QUART:(c + 1) * QUART], bank(7), xf_copied, scale=rowsT[:, 10:11],
                     bias=rowsT[:, 11:12])
                act.wait_ge(ssq_done, c + 1)
                if c:
                    act.wait_ge(xqk_ready, 2 * c)
                for k, n in ((0, HEADS * HD), (1, KV * HD)):
                    act.activation(gx[:, 2 + k, :], bank(4 + k), ACT.Sqrt, scale=1.0 / n,
                                   bias=cst[:, 2:3]).then_inc(act_mean, 1)

            def exps(t, u, a, b):
                for s in range(a, b):
                    last = act.activation(sp[:, u, s, :], sp[:, u, s, :], ACT.Exp, bias=z0[:, u, 0, s:s + 1],
                                          accum_out=z0[:, u, 1, s:s + 1])
                return last

            def copy_pT(t, h):
                act.wait_ge(pT_done, t * 2 + h + 1)
                if later(t):
                    act.wait_ge(y_done, t * 2 + h - 1)
                copy(pTs[:, h, 0:4, :].rearrange("p a b -> p (a b)"), bank(4), pTa_copied)

            def step(t, u):
                v = 1 - u
                if has(t):
                    act.wait_ge(q_done, t + 1)
                    if later(t, 1):
                        act.wait_ge(scores_done, (t - 1) * 2)
                    copy(qs[:, u].rearrange("p a b -> p (a b)"), bank(0, 2), q_copied)
                    act.wait_ge(kv_done, t + 1)
                    if later(t, 1):
                        act.wait_ge(y_done, (t - 1) * 2)
                    copy(vs[:, u].rearrange("p a b -> p (a b)"), bank(3), v_copied)
                if has(t, 1):
                    copy_pT(t - 1, 0)
                if has(t, 2):
                    act.wait_ge(xT_done, t - 1)
                    act.activation(xn1T[:, tok(t - 2)], ps[:, 7, 0:P], ACT.Identity,
                                   accum_out=xsum[:, bass.ds(t - 2, 1)]).then_inc(xn1T_copied, 1)
                if has(t, 1):
                    act.wait_ge(y_done, (t - 1) * 2 + 1)
                    if later(t - 1, 1):
                        act.wait_ge(x1_done, t - 2)
                    copy(yTs[:, v, 0:4, :].rearrange("p j (b q) -> p b j q", b=2),
                         ps[:, 6, :].rearrange("p (b j q) -> p b j q", b=2, j=4), ya_copied)
                if has(t):
                    act.wait_ge(nmax_ready, t * 2 + 1)
                    if later(t, 1):
                        act.wait_ge(probs_ready, (t - 1) * 2)
                    exps(t, u, 0, 4)
                if has(t, 1):
                    copy_pT(t - 1, 1)
                if has(t):
                    exps(t, u, 4, 8).then_inc(exp_done, 1)
                if has(t, 2):
                    act.wait_ge(qkv_done, t - 1)
                    act.activation(vT[:, tok(t - 2)], ps[:, 7, 3 * P:4 * P], ACT.Identity)
                    if later(t - 2, 1):
                        act.wait_ge(scr_w[u], (t - 2 - u) * 32)
                    copy(parts[:, u, 0].rearrange("p a b -> p (a b)"), ps[:, 7, P:3 * P], p1_ready)
                if has(t):
                    act.wait_ge(nmax_ready, t * 2 + 2)
                    exps(t, u, 8, 16).then_inc(exp_done, 1)

            tiles(act, step, 2)

            def combine_exp(t):
                act.wait_ge(comb, t * 5 + 1)
                act.activation(fT[:, 2, :], fT[:, 1, :], ACT.Exp).then_inc(comb_e, 1)

            def hidden(t, g):
                act.wait_ge(h_done, t * 2 + g + 1)
                if later(t):
                    act.wait_ge(ffn_done, t * 2)
                b = 2 * (AT["AB"[g]] % BUFS)
                for n in range(2):
                    f = 2 * g + n
                    last = act.activation(hT[:, f, :], ps[:, b, n * P:(n + 1) * P], ACT.Relu, bias=c1T[:, f:f + 1])
                last.then_inc(h_ready, 1)

            def attend(t, lagged):
                for p, turn in enumerate(TURNS):
                    if isinstance(turn, tuple):
                        h, c = turn
                        i = h * NS + c
                        act.wait_ge(l_max, t * NC + i + 1)
                        b = 2 * (p % BUFS)
                        col = lambda a: a[:, bass.ds(t, 1), i:i + 1].rearrange("p a b -> p (a b)")
                        act.activation(bank(b, 2), bank(b, 2), ACT.Exp, bias=col(lnm), accum_out=col(lz)
                                       ).then_inc(l_slots, 1)
                    if lagged and p == 3:
                        combine_exp(t - 1)
                    if turn in ("A", "B"):
                        hidden(t, "AB".index(turn))

            attend(0, False)
            with act.Fori(1, T) as t:
                attend(t, True)
            combine_exp(T - 1)

        @block.vector
        def _(dve):
            bank = lambda b, n=1: ps[:, b:b + n, :].rearrange("p b n -> p (b n)")

            for c in range(NQ):
                ts = range(c * TQ, (c + 1) * TQ)
                tt = slice(c * TQ, (c + 1) * TQ)
                n = 20 * c
                dve.wait_ge(x_in[c], 16)
                for t in ts:
                    dve.bn_stats(st[:, t, :], xs[:, t, :]).then_inc(dve_pro, 1)
                dve.wait_ge(dve_pro, n + 4)
                for t in ts:
                    dve.bn_aggr(mv[:, t, :], st[:, t, :]).then_inc(dve_pro, 1)
                dve.wait_ge(dve_pro, n + 8)
                dve.tensor_scalar(mv[:, tt, 1], mv[:, tt, 1], 1e-5, None, ALU.add).then_inc(dve_pro, 4)
                dve.wait_ge(pool_pro, 2 * c + 1)
                for t in ts:
                    dve.tensor_scalar(x1[:, t, :], xs[:, t, :], mv[:, t, 0:1], rstd[:, t:t + 1], ALU.subtract,
                                      ALU.mult).then_inc(xn_ready, 1)
                dve.wait_ge(xn_ready, 4 * (c + 1))
                for t in ts:
                    dve.bn_stats(st2[:, t, :], x1[:, t, :]).then_inc(dve_pro, 1)
                dve.wait_ge(dve_pro, n + 16)
                for t in ts:
                    last = dve.bn_aggr(mv2[:, t, :], st2[:, t, :])
                last.then_inc(dve_pro, 3)
                dve.wait_ge(dve_pro, n + 19)
                dve.tensor_scalar(mv2[:, tt, 1], mv2[:, tt, 1], 1e-3, None, ALU.add).then_inc(dve_pro, 1)
                dve.wait_ge(pool_pro, 2 * c + 2)
                for t in ts:
                    dve.tensor_scalar(xn2[:, t, :], x1[:, t, :], mv2[:, t, 0:1], rstd2[:, t:t + 1],
                                      ALU.subtract, ALU.mult).then_inc(xn2_ready, 1)
                if c == 0:
                    dve.wait_ge(act_pro, 1)
                    dve.wait_ge(wa_in, 16 * NWA)
                    dve.tensor_tensor(wq_s, wq_nat, rowsT[:, 0:CH].unsqueeze(2).broadcast_to([P, CH, C]),
                                      ALU.mult).then_inc(wqk_scaled, 1)
                    dve.wait_ge(wb_in, 16 * NWB)
                    dve.tensor_copy(optT[:].rearrange("p (d h) -> p d h", d=D1),
                                    w_nat[:, 3, :].rearrange("p (h d) -> p d h", d=D1)).then_inc(wqk_scaled, 1)
                    dve.tensor_tensor(wk_s[:], w_kv[:, 0:2, :], rowsT[:, 8:10].unsqueeze(2).broadcast_to([P, 2, C]),
                                      ALU.mult).then_inc(wqk_scaled, 1)
            dve.wait_ge(wb_in, 16 * NWB)
            dve.tensor_reduce(fsc[:, 0:1], tern[:], AX.X, ALU.add, apply_absolute_value=True).then_inc(wabs_ready, 1)
            for c in range(NQ):
                cs = slice(c * QUART, (c + 1) * QUART)
                cp = slice(BLK + c * QUART, BLK + (c + 1) * QUART)
                for k in (0, 1):
                    dve.wait_ge(gx_done, 2 * c + k + 1)
                    if c:
                        dve.wait_ge(ssq_done, c)
                    dve.tensor_tensor(gx[:, k, :], xnT[:, cp], bank(2 + k), ALU.mult).then_inc(gx_ready, 1)
                dve.wait_ge(act_mean, 2 * c + 2)
                for k in (0, 1):
                    dve.reciprocal(gx[:, 2 + k, :], gx[:, 2 + k, :]).then_inc(rms_ready, 1)
                dve.wait_ge(rms_ready, 2 * c + 1)
                dve.tensor_tensor(xqT[:, cs], xnT[:, cp], gx[:, 2, :], ALU.mult).then_inc(xqk_ready, 1)
                dve.wait_ge(rms_ready, 2 * c + 2)
                dve.tensor_tensor(xkT[:, cp], xnT[:, cp], gx[:, 3, :], ALU.mult).then_inc(xqk_ready, 1)
                dve.wait_ge(xf_copied, c + 1)
                dve.tensor_reduce(fsc[:, 1 + c:2 + c], xfT[:, cs], AX.X, ALU.max,
                                  apply_absolute_value=True).then_inc(amax_ready, 1)
            dve.wait_ge(amax_ready, NQ)
            dve.tensor_reduce(fsc[:, 5:6], fsc[:, 1:5], AX.X, ALU.max).then_inc(amax_ready, 1)
            dve.wait_ge(pe_pro, 7)
            dve.tensor_scalar(fsc[:, 10:11], ps[:, 6, 0:1], 1.0 / (C * C), None, ALU.mult).then_inc(tern_step, 1)
            dve.wait_ge(tern_step, 1)
            dve.tensor_scalar(fsc[:, 11:12], fsc[:, 10:11], 1e-5, None, ALU.add).then_inc(tern_step, 1)
            dve.wait_ge(tern_step, 2)
            dve.reciprocal(fsc[:, 12:13], fsc[:, 11:12]).then_inc(tern_step, 1)
            dve.wait_ge(tern_step, 3)
            dve.tensor_scalar(tern[:], tern[:], fsc[:, 12:13], ROUND, ALU.mult, ALU.add).then_inc(tern_step, 1)
            dve.wait_ge(tern_step, 4)
            dve.tensor_scalar(tern[:], tern[:], ROUND, 1.0, ALU.subtract, ALU.min).then_inc(tern_step, 1)
            dve.wait_ge(tern_step, 5)
            dve.tensor_scalar(tern[:], tern[:], -1.0, None, ALU.max).then_inc(tern_step, 1)
            dve.wait_ge(gmax_ready, 1)
            dve.reciprocal(fsc[:, 7:8], fsc[:, 6:7]).then_inc(fsc_ready, 1)
            dve.tensor_scalar(fsc[:, 13:14], fsc[:, 6:7], 1.0 / 128.0, None, ALU.mult).then_inc(fsc_ready, 1)
            dve.wait_ge(fsc_ready, 2)
            dve.tensor_scalar(fsc[:, 8:9], fsc[:, 7:8], 128.0, None, ALU.mult).then_inc(fsc_ready, 1)
            dve.tensor_tensor(fsc[:, 9:10], fsc[:, 13:14], fsc[:, 10:11], ALU.mult).then_inc(fsc_ready, 2)
            dve.wait_ge(fsc_ready, 5)
            dve.wait_ge(bias_in, 16)

            def ffn_input(t, u):
                if later(t, 1):
                    dve.wait_ge(x1_done, t - 1)
                dve.tensor_scalar(ffx[:, u, 0, :], xfT[:, tok(t)], fsc[:, 8:9], LIM, ALU.mult,
                                  ALU.min).then_inc(ffx_step, 1)
                dve.wait_ge(ffx_step, t + 1)
                dve.tensor_scalar(ffx[:, u, 1, :], ffx[:, u, 0, :], -LIM, fsc[:, 9:10], ALU.max,
                                  ALU.mult).then_inc(ffx_ready, 1)

            def add_bias(t, u, h):
                dve.wait_ge(scores_done, t * 2 + h + 1)
                if later(t, 1):
                    dve.wait_ge(pT_done, (t - 1) * 2)
                for r in (0, 1):
                    s = 8 * h + 4 * r
                    bv = biasm[:, 4 * h + 2 * r:4 * h + 2 * r + 2, :].rearrange("p a b -> p (a b)")
                    last = dve.tensor_tensor(sp[:, u, s:s + 4, :].rearrange("p (b a) n -> p b (a n)", b=2),
                                             ps[:, 2 * h + r, :].rearrange("p (b n) -> p b n", b=2),
                                             bv.unsqueeze(1).broadcast_to([P, 2, 2 * P]), ALU.add)
                last.then_inc(bias_added, 1)
                dve.wait_ge(bias_added, t * 2 + h + 1)
                if isinstance(t, int) and t == 0:
                    for r in (0, 1):
                        s = 8 * h + 4 * r
                        last = dve.memset(sp[:, u, s:s + 2, 0:BLK], BIG)
                    last.then_inc(first_masked, 1)

            def row_max(t, u, h):
                if isinstance(t, int) and t == 0:
                    dve.wait_ge(first_masked, h + 1)
                hs = slice(8 * h, 8 * h + 8)
                dve.tensor_reduce(z0[:, u, 0, hs], sp[:, u, hs, :], AX.X, ALU.max,
                                  negate=True).then_inc(nmax_ready, 1)

            def copy_pT(t, h):
                dve.wait_ge(pT_done, t * 2 + h + 1)
                if later(t):
                    dve.wait_ge(y_done, t * 2 + h - 1)
                dve.tensor_copy(pTs[:, h, 4:8, :].rearrange("p a b -> p (a b)"), bank(5)).then_inc(pTd_copied, 1)

            def step(t, u):
                v = 1 - u
                if has(t):
                    dve.wait_ge(kv_done, t + 1)
                    if later(t, 1):
                        dve.wait_ge(scores_done, (t - 1) * 2)
                    dve.tensor_copy(ks[:, u].rearrange("p a b -> p (a b)"), ps[:, 2, 0:2 * WIN]).then_inc(k_copied, 1)
                if has(t, 2):
                    dve.wait_ge(x1_done, t - 1)
                    dve.tensor_tensor(x1[:, bass.ds(t - 2, 1), :].rearrange("p a c -> p (a c)"),
                                      xs[:, bass.ds(t - 2, 1), :].rearrange("p a c -> p (a c)"),
                                      ps[:, 7, 0:C], ALU.add).then_inc(x1_ready, 1)
                    dve.wait_ge(bias_in, 16)
                    dve.wait_ge(x1_ready, t - 1)
                    dve.bn_stats(st3[:, u, :], x1[:, bass.ds(t - 2, 1), :].rearrange("p a c -> p (a c)")).then_inc(st_ready, 1)
                    dve.wait_ge(bias_in, 16)
                    dve.wait_ge(st_ready, t - 1)
                    dve.bn_aggr(mv3[:, u, :], st3[:, u, :]).then_inc(mv_ready, 1)
                    dve.wait_ge(mv_ready, (t - 2) * 2 + 1)
                    dve.tensor_scalar(mv3[:, u, 1:2], mv3[:, u, 1:2], 1e-5, None, ALU.add).then_inc(mv_ready, 1)
                if has(t, 1):
                    copy_pT(t - 1, 0)
                if has(t, 2):
                    dve.wait_ge(rstd_ready, t - 1)
                    if later(t - 2, 1):
                        dve.wait_ge(xT_done, t - 3)
                    dve.tensor_scalar(xn1[:, u, :], x1[:, bass.ds(t - 2, 1), :].rearrange("p a c -> p (a c)"), mv3[:, u, 0:1],
                                      rstd3[:, u:u + 1], ALU.subtract, ALU.mult).then_inc(xn1_ready, 1)
                if has(t):
                    add_bias(t, u, 0)
                    row_max(t, u, 0)
                    add_bias(t, u, 1)
                if has(t, 1):
                    copy_pT(t - 1, 1)
                if has(t):
                    row_max(t, u, 1)
                if has(t, 1):
                    ffn_input(t - 1, v)
                if has(t, 1):
                    dve.wait_ge(y_done, t * 2)
                    if later(t - 1, 1):
                        dve.wait_ge(x1_done, t - 2)
                    dve.tensor_copy(yTs[:, v, 4:8, :].rearrange("p j (b q) -> p b j q", b=2),
                                    ps[:, 6, :].rearrange("p (b j q) -> p b j q", b=2, j=4)).then_inc(yd_copied, 1)
                if has(t, 2):
                    dve.wait_ge(p1_ready, t - 1)
                    if later(t - 2, 1):
                        dve.wait_ge(split_ready, t - 3)
                    dve.tensor_tensor(rem[:, u].rearrange("p a b -> p (a b)"), ps[:, 7, P:3 * P],
                                      parts[:, u, 0].rearrange("p a b -> p (a b)"), ALU.subtract).then_inc(rem_ready, 1)

            tiles(dve, step, 2)

            dve.wait_ge(xn1T_copied, T)
            dve.tensor_reduce(xsum[:, T:T + 1], xsum[:, 0:T], AX.X, ALU.add).then_inc(gate_step, 1)
            dve.wait_ge(gate_pe, 1)
            dve.scalar_tensor_tensor(gate[:, 0, :], ps[0:1, 6, 0:EXPERTS], 1.0 / S, br_s[:], ALU.mult,
                                     ALU.add).then_inc(gate_step, 1)
            dve.wait_ge(gate_step, 2)
            dve.max(gate[:, 1, :], gate[:, 0, :]).then_inc(gate_step, 1)
            dve.wait_ge(gate_step, 3)
            dve.max_index(gidx[:], gate[:, 1, :], gate[:, 0, :]).then_inc(gate_step, 1)

            def row_maxima(t):
                dve.wait_ge(l_max, (t + 1) * NC)
                if later(t):
                    dve.wait_ge(comb, t * 5)
                dve.tensor_reduce(fT[:, 0, 0:H1], lnm[:, bass.ds(t, 1), :].rearrange("p a (h s) -> p (a h) s", s=NS),
                                  AX.X, ALU.min).then_inc(mn_ready, 1)

            def weigh(t):
                dve.wait_ge(f_done, t + 1)
                if later(t):
                    dve.wait_ge(o_done, t)
                dve.tensor_tensor(optT[:], vT[:, tok(t)], ps[:, 2 * (AT["A"] % BUFS) + 1, 0:P], ALU.mult
                                  ).then_inc(opt_ready, 1)

            def finish(t):
                dve.wait_ge(o_done, t + 1)
                dve.wait_ge(ffn_added, (t + 1) * 2)
                xv = x1[:, bass.ds(t, 1), :].rearrange("p a c -> p (a c)")
                dve.tensor_tensor(xv, xv, ps[:, 2 * (AT["B"] % BUFS) + 1, 0:C], ALU.add).then_inc(o_ready, 1)

            def add_ffn(t, g):
                dve.wait_ge(ffn_done, t * 2 + g + 1)
                if g:
                    dve.wait_ge(ffn_added, t * 2 + 1)
                elif not later(t):
                    dve.wait_ge(biased, 2)
                xv = x1[:, bass.ds(t, 1), :].rearrange("p a c -> p (a c)")
                dve.tensor_tensor(xv, xv, ps[:, 2 * (AT["CD"[g]] % BUFS), 0:C], ALU.add).then_inc(ffn_added, 1)

            def maxima(t, lagged):
                for p, turn in enumerate(TURNS):
                    if isinstance(turn, tuple):
                        h, c = turn
                        i = h * NS + c
                        dve.wait_ge(l_scores, t * NC + i + 1)
                        dve.tensor_reduce(lnm[:, bass.ds(t, 1), i:i + 1].rearrange("p a b -> p (a b)"),
                                          bank(2 * (p % BUFS), 2), AX.X, ALU.max, negate=True).then_inc(l_max, 1)
                    if lagged and p == 1:
                        row_maxima(t - 1)
                    if lagged and turn == "A":
                        weigh(t - 1)
                    if lagged and turn == "B":
                        finish(t - 1)
                    if turn in ("C", "D"):
                        add_ffn(t, "CD".index(turn))

            maxima(0, False)
            with dve.Fori(1, T) as t:
                maxima(t, True)
            row_maxima(T - 1)
            weigh(T - 1)
            finish(T - 1)

        @block.tensor
        def _(pe):
            pe.wait_ge(consts, 9)
            pe.wait_ge(wa_in, 16 * NWA)
            pe.wait_ge(wb_in, 16 * NWB)
            pe.transpose(ps[:, 7, 0:12], rows[:], ident[0:12, 0:12]).then_inc(pe_pro, 1)
            for j in range(CH):
                pe.matmul(ps[:, 6, 0:C], wq_nat[:, j, :], wq_nat[:, j, :], start=(j == 0), stop=(j == CH - 1))
            for j in range(2):
                last = pe.matmul(ps[:, 6, C:2 * C], w_kv[:, j, :], w_kv[:, j, :], start=(j == 0), stop=(j == 1))
            last.then_inc(pe_pro, 1)
            pe.wait_ge(wqk_scaled, 3)
            for j in range(CH):
                last = pe.transpose(ps[:, j // 4, (j % 4) * P:(j % 4 + 1) * P], wq_s[:, j, :], ident[:])
            last.then_inc(pe_pro, 1)
            for j in range(2):
                pe.transpose(ps[:, 2, j * P:(j + 1) * P], wk_s[:, j, :], ident[:])
            for j in range(2, 4):
                last = pe.transpose(ps[:, 2, j * P:(j + 1) * P], w_kv[:, j, :], ident[:])
            last.then_inc(pe_pro, 1)
            for j in range(CH):
                last = pe.transpose(ps[:, 3 + j // 4, (j % 4) * P:(j % 4 + 1) * P], wo_nat[:, j].rearrange("p r d -> p (r d)"), ident[:])
            last.then_inc(pe_pro, 1)
            for j in range(4):
                last = pe.transpose(ps[:, 5, j * P:(j + 1) * P],
                                    w_nat[:, j, :] if j < 3 else optT[:],
                                    ident[:])
            last.then_inc(pe_pro, 1)
            pe.wait_ge(act_pro, 2)
            pe.wait_ge(wabs_ready, 1)
            pe.matmul(ps[:, 6, 0:1], ones[:], fsc[:, 0:1], start=True, stop=True).then_inc(pe_pro, 1)
            pe.wait_ge(act_pro, 6)
            for c in range(NQ):
                ts = range(c * TQ, (c + 1) * TQ)
                pe.wait_ge(xn_ready, 4 * (c + 1))
                for j, t in enumerate(ts):
                    last = pe.transpose(ps[:, c % 2, j * P:(j + 1) * P], x1[:, t, :], ident[:])
                last.then_inc(xnT_done, 1)
                pe.wait_ge(xn2_ready, 4 * (c + 1))
                if c:
                    pe.wait_ge(xf_copied, c)
                for j, t in enumerate(ts):
                    last = pe.transpose(ps[:, 7, j * P:(j + 1) * P], xn2[:, t, :], ident[:])
                last.then_inc(xfT_done, 1)
                pe.wait_ge(xn_copied, c + 1)
                if c:
                    pe.wait_ge(gx_ready, 2 * c)
                cp = slice(BLK + c * QUART, BLK + (c + 1) * QUART)
                for k in (0, 1):
                    pe.matmul(ps[:, 2 + k, :], gram[:, k, :], xnT[:, cp], start=True, stop=True).then_inc(gx_done, 1)
                pe.wait_ge(gx_ready, 2 * (c + 1))
                if c:
                    pe.wait_ge(act_mean, 2 * c)
                for k in (0, 1):
                    last = pe.matmul(ps[:, 4 + k, :], ones[:], gx[:, k, :], start=True, stop=True)
                last.then_inc(ssq_done, 1)

            def project(t, u):
                pe.wait_ge(win_ready, t + 1)
                if later(t):
                    pe.wait_ge(bias_added, t * 2)
                qv = ps[:, 0:2, :].rearrange("p c (g b a q) -> p c g a b q", g=2, b=2, a=2)
                for j in range(CH):
                    last = pe.matmul(qv[:, j // 4, j % 4 // 2, j % 2], wqT[:, j, :], xqT[:, tok(t)],
                                     start=True, stop=True)
                last.then_inc(q_done, 1)
                for j in range(2):
                    pe.matmul(ps[:, 2, j * WIN:(j + 1) * WIN], wkvT[:, j, :], xkT[:, bass.ds(t * P, WIN)],
                              start=True, stop=True)
                for b in range(2):
                    last = pe.matmul(ps[:, 3, b * 2 * C:(b + 1) * 2 * C], win[:, u, b * BLK:b * BLK + P],
                                     wkvT[:, 2:4, :].rearrange("p a b -> p (a b)"), start=True, stop=True)
                last.then_inc(kv_done, 1)

            def scores(t, u, h):
                pe.wait_ge(q_copied, t + 1)
                pe.wait_ge(k_copied, t + 1)
                if h:
                    pe.wait_ge(v_copied, t + 1)
                for b in range(2):
                    for a in range(2):
                        for r in range(2):
                            rr = slice(r * HD, (r + 1) * HD)
                            last = pe.matmul(ps[:, 2 * h + r, (2 * b + a) * P:(2 * b + a + 1) * P],
                                             qs[rr, u, 4 * h + 2 * a + b, :],
                                             ks[rr, u, h, b * BLK:b * BLK + P], start=True, stop=True)
                last.then_inc(scores_done, 1)

            def transpose_probs(t, u, h):
                pe.wait_ge(probs_ready, t * 2 + h + 1)
                if later(t) or h:
                    pe.wait_ge(pTa_copied, t * 2 + h)
                    pe.wait_ge(pTd_copied, t * 2 + h)
                for s in range(8):
                    last = pe.transpose(ps[:, 4 + s // 4, (s % 4) * P:(s % 4 + 1) * P], sp[:, u, 8 * h + s, :], ident[:])
                last.then_inc(pT_done, 1)

            def values(t, u, h):
                pe.wait_ge(pTa_copied, t * 2 + h + 1)
                pe.wait_ge(pTd_copied, t * 2 + h + 1)
                if h:
                    pe.wait_ge(ya_copied, t + 1)
                elif later(t):
                    pe.wait_ge(yd_copied, t)
                else:
                    pe.wait_ge(tern_step, 1)
                for b in range(2):
                    for r in range(2):
                        g = 2 * h + r
                        last = pe.matmul(ps[r * HD:(r + 1) * HD, 6, b * 256:(b + 1) * 256],
                                         vs[:, u, b, g * HD:(g + 1) * HD],
                                         pTs[:, h, 4 * r + 2 * b:4 * r + 2 * b + 2, :].rearrange("p a b -> p (a b)"),
                                         start=True, stop=True)
                last.then_inc(y_done, 1)

            def project_out(t, u):
                pe.wait_ge(ya_copied, t + 1)
                pe.wait_ge(yd_copied, t + 1)
                pe.wait_ge(ffx_ready, t + 1)
                if later(t):
                    pe.wait_ge(rem_ready, t)
                elif isinstance(t, int):
                    pe.wait_ge(tern_step, 6)
                for j in range(CH):
                    pe.matmul(ps[:, 7, 0:C], yTs[:, u, j, :], woT[:, j, :], start=(j == 0), stop=False)
                pe.matmul(ps[:, 7, 0:C], ffx[:, u, 1, :], tern[:], start=False, stop=True).then_inc(x1_done, 1)

            def step(t, u):
                v = 1 - u
                if has(t):
                    if isinstance(t, int) and t == 0:
                        pe.wait_ge(xqk_ready, 2 * NQ)
                        pe.wait_ge(act_pro, 7)
                        pe.wait_ge(act_mean, 2 * NQ)
                        pe.wait_ge(xf_copied, NQ)
                    project(t, u)
                if has(t, 2):
                    project_out(t - 2, u)
                if has(t, 1):
                    transpose_probs(t - 1, v, 0)
                if has(t):
                    scores(t, u, 0)
                    scores(t, u, 1)
                if has(t, 2):
                    pe.wait_ge(xn1_ready, t - 1)
                    pe.transpose(ps[:, 7, 0:P], xn1[:, u, :], ident[:]).then_inc(xT_done, 1)
                if has(t, 1):
                    values(t - 1, v, 0)
                    transpose_probs(t - 1, v, 1)
                if has(t, 2):
                    pe.wait_ge(xn1T_copied, t - 1)
                    for s in range(3):
                        o = ps[:, 7, (s + 1) * P:(s + 2) * P]
                        pe.matmul(o, w_inT[:, s].rearrange("p d h -> p (d h)"), xn1T[:, tok(t - 2)],
                                  start=True, stop=False)
                        last = pe.matmul(o, bin_row[:, s].rearrange("p d h -> p (d h)"), ones[0:1, :],
                                         start=False, stop=True)
                    last.then_inc(qkv_done, 1)
                if has(t, 1):
                    values(t - 1, v, 1)

            tiles(pe, step, 2)

            pe.wait_ge(gate_step, 1)
            pe.matmul(ps[0:1, 6, 0:EXPERTS], xsum[:, T:T + 1], wr_s[:], start=True, stop=True).then_inc(gate_pe, 1)

            def replicate(t):
                pe.wait_ge(comb, t * 5 + 5)
                pe.matmul(ps[:, 2 * (AT["A"] % BUFS) + 1, 0:P], frep[:], ident[:], start=True, stop=True
                          ).then_inc(f_done, 1)

            def attn_out(t):
                pe.wait_ge(opt_ready, t + 1)
                pe.matmul(ps[:, 2 * (AT["B"] % BUFS) + 1, 0:C], optT[:], w_outT[:], start=True, stop=True
                          ).then_inc(o_done, 1)

            def hidden(t, g):
                for n in range(2):
                    f = 2 * g + n
                    last = pe.matmul(ps[:, 2 * (AT["AB"[g]] % BUFS), n * P:(n + 1) * P], w1e[:, f:FF:FC],
                                     xn1T[:, tok(t)], start=True, stop=True)
                last.then_inc(h_done, 1)

            def expert_out(t, g):
                pe.wait_ge(h_ready, t * 2 + g + 1)
                for n in range(2):
                    f = 2 * g + n
                    last = pe.matmul(ps[:, 2 * (AT["CD"[g]] % BUFS), 0:C], hT[:, f, :], w2e[:, f, :],
                                     start=(n == 0), stop=(n == 1))
                last.then_inc(ffn_done, 1)

            def wait_free(p, t, first, lagged):
                q, s, lg = p - BUFS, t, lagged
                if q < 0:
                    if first:
                        return
                    q, s, lg = q + len(TURNS), t - 1, True
                user = TURNS[q]
                if isinstance(user, tuple):
                    pe.wait_ge(l_slots, s * NC + (user[0] * NS + user[1] + 1))
                elif user in "CD":
                    pe.wait_ge(ffn_added, s * 2 + (1 + "CD".index(user)))
                else:
                    pe.wait_ge(h_ready, s * 2 + (1 + "AB".index(user)))
                    if lg:
                        pe.wait_ge(opt_ready if user == "A" else o_ready, s)

            def attend(t, first, lagged):
                for p, turn in enumerate(TURNS):
                    b = 2 * (p % BUFS)
                    wait_free(p, t, first, lagged)
                    if isinstance(turn, tuple):
                        h, c = turn
                        if h % 8 == 0 and c == 0:
                            pe.wait_ge(q_in[h // 8], (t + 1) * 16)
                        if first and h == 0:
                            pe.wait_ge(kst_in[3] if c else kst_in[0], 48 if c else 16 * 3 * (NQ - 1))
                        for n in range(2):
                            q = 2 * c + n
                            rhs = kst[:, q, h, :] if q < 3 else kst3[0:ROWS, h, :]
                            last = pe.matmul(ps[:, b + n, :], qst[0:ROWS, h, :], rhs, start=True, stop=True)
                        last.then_inc(l_scores, 1)
                    if turn == "A" and first:
                        pe.wait_ge(exp_in, 64)
                    if turn in ("A", "B"):
                        hidden(t, "AB".index(turn))
                    if turn == "A" and lagged:
                        replicate(t - 1)
                    if turn == "B" and lagged:
                        attn_out(t - 1)
                    if turn in ("C", "D"):
                        expert_out(t, "CD".index(turn))

            pe.wait_ge(rem_ready, T)
            pe.wait_ge(exp_done, 2 * T)
            pe.wait_ge(gate_step, 2)
            pe.wait_ge(bias_added, 2 * T)
            pe.wait_ge(pTa_copied, 2 * T)
            pe.wait_ge(pTd_copied, 2 * T)
            attend(0, True, False)
            with pe.Fori(1, T) as t:
                attend(t, False, True)
            pe.wait_ge(l_slots, T * NC)
            replicate(T - 1)
            attn_out(T - 1)


_INS = ["L0_attn_x", "L0_attn_wq", "L0_attn_wk", "L0_attn_wv", "L0_attn_wo", "L0_attn_q_norm_w", "L0_attn_k_norm_w",
        "L0_ffn_weight", "L0_ffn_ln_gamma", "L0_ffn_ln_beta", "L1_attn_w_in", "L1_attn_b_in", "L1_attn_w_out",
        "L1_attn_b_out", "L1_ffn_Wr", "L1_ffn_br", "L1_ffn_W1", "L1_ffn_b1", "L1_ffn_W2", "L1_ffn_b2"]


def alibi_table():
    import numpy as _np
    slopes = _np.array([(2.0 ** (-8.0 / HEADS)) ** (i + 1) for i in range(HEADS)], dtype=_np.float32)
    rel = _np.arange(P)[None, :] - BLK - _np.arange(BLK)[:, None]
    seen = (rel <= 0) & (rel >= -BLK)
    tab = _np.zeros((2, BLK, 8, P), _np.float32)
    for a in range(2):
        for s in range(8):
            cph, r, cpl = s // 4, s // 2 % 2, s % 2
            tab[a, :, s, :] = _np.where(seen, slopes[head_of(cph, r, 2 * cpl + a)] * rel.astype(_np.float32), BIG)
    return tab.reshape(P, 8, P)


def kernel(**inputs):
    import numpy as _np
    import concourse.bacc as _bacc
    from concourse import mybir as _mybir
    from concourse.bass_utils import run_bass_kernel_spmd as _run

    nc = _bacc.Bacc("TRN2", target_bir_lowering=False, num_devices=1)
    arrays, args = {}, []
    named = [(n, _np.ascontiguousarray(inputs[n])) for n in _INS] + [("alibi", alibi_table())]
    for name, a in named:
        arrays[f"in_{name}"] = a
        args.append(nc.dram_tensor(f"in_{name}", a.shape, _mybir.dt.from_np(a.dtype), kind="ExternalInput").ap())
    shape = inputs["L0_attn_x"].shape
    args.append(nc.dram_tensor("out_0", shape, _mybir.dt.float32, kind="ExternalOutput").ap())
    two_layers(nc, *args)
    r = _run(nc, [arrays], core_ids=[0])
    return r.results[0]["out_0"]
```

```python
from contextlib import ExitStack

import concourse.bass as bass
from concourse import mybir

F32 = mybir.dt.float32
BF16 = mybir.dt.bfloat16
U32 = mybir.dt.uint32
ALU = mybir.AluOpType
ACT = mybir.ActivationFunctionType
AX = mybir.AxisListType
RMAX = bass.bass_isa.ReduceOp.max

P = 128
C = 128
HEADS, KV, HD = 16, 4, 64
BLK = 64
CH = HEADS * HD // P
H1, D1 = 16, 8
PAIRS = ((0, 0), (0, 1), (0, 2), (1, 0), (1, 1), (2, 0))
ROWS = len(PAIRS) * D1
QUART = 512
NS, BUFS = 2, 4
OTHERS = {14: "A", 20: "C", 26: "B", 32: "D"}
HALVES = [(h, s) for s in range(NS) for h in range(H1)]
NC = len(HALVES)
TURNS = list(HALVES)
for _p in sorted(OTHERS):
    TURNS.insert(_p, OTHERS[_p])
AT = {v: k for k, v in OTHERS.items()}
EARLY = 8
EXPERTS, FF = 8, 512
FC = FF // P
BIG = -1e30
ROUND = 1.5 * 2.0 ** 23
LIM = 128.0 - 1e-5


def head_of(cph, r, j):
    return cph * 8 + r * 4 + j


def two_layers(nc, x, wq, wk, wv, wo, q_norm_w, k_norm_w, ffn_w, ln_gamma, ln_beta,
               w_in, b_in, w_out, b_out, Wr, br, W1, b1, W2, b2, alibi, out):
    _, S, _ = x.shape
    T = S // P
    NQ = S // QUART
    TQ = QUART // P

    with ExitStack() as ctx:
        def sb(name, shape, dt=F32):
            return ctx.enter_context(nc.sbuf_tensor(name, shape, dt))

        def sem(name):
            return ctx.enter_context(nc.semaphore(name))

        ps = ctx.enter_context(nc.psum_tensor("ps", [P, 8, 512], F32))

        ident = sb("ident", [P, P])
        ones = sb("ones", [P, P])
        cst = sb("cst", [P, 4])
        rows = sb("rows", [12, P])
        rowsT = sb("rowsT", [P, 12])
        w_kv = sb("w_kv", [P, 4, C])
        wk_s = sb("wk_s", [P, 2, C])
        gram = sb("gram", [P, 2, C])
        wqT = sb("wqT", [C, CH, P])
        wkvT = sb("wkvT", [C, 4, P])
        woT = sb("woT", [P, CH, C])
        tern = sb("tern", [C, C])
        w_inT = sb("w_inT", [C, 3, D1, H1])
        w_outT = sb("w_outT", [P, C])
        bin_nat = sb("bin_nat", [1, 3 * C])
        bin_row = sb("bin_row", [1, 3, D1, H1])
        outb = sb("outb", [P, 3, C])
        c1T = sb("c1T", [P, FC])
        wr_s = sb("wr_s", [C, EXPERTS])
        br_s = sb("br_s", [1, EXPERTS])
        gate = sb("gate", [1, 3, EXPERTS])
        gidx = sb("gidx", [1, EXPERTS], U32)
        xsum = sb("xsum", [C, T + 1])
        st = sb("st", [P, T, 6])
        mv = sb("mv", [P, T, 2])
        rstd = sb("rstd", [P, T])
        st2 = sb("st2", [P, T, 6])
        mv2 = sb("mv2", [P, T, 2])
        rstd2 = sb("rstd2", [P, T])
        nmean2 = sb("nmean2", [P, T])
        st3 = sb("st3", [P, 2, 6])
        mv3 = sb("mv3", [P, 2, 2])
        rstd3 = sb("rstd3", [P, 2])
        fsc = sb("fsc", [P, 16])
        ms = sb("ms", [P, T, 2])
        rqk = sb("rqk", [P, T, 2])
        binT = sb("binT", [P, 3])
        xs = sb("xs", [P, T, C])
        x1 = sb("x1", [P, T, C])
        xnT = sb("xnT", [C, S])
        xkT = sb("xkT", [C, S])
        xqf = sb("xqf", [C, 2, S])
        xqT, xfT = xqf[:, 0, :], xqf[:, 1, :]
        biasm = sb("biasm", [P, 2, 8, P])
        qs = sb("qs", [P, 2, CH, P])
        ks = sb("ks", [P, 2, 2, 2, P])
        vs = sb("vs", [P, 2, 2, 2 * C])
        win = sb("win", [C, 2, P])
        ffx = sb("ffx", [C, 2, 2, P])
        sp = sb("sp", [P, 2, 16, P])
        z0 = sb("z0", [P, 2, 3, 16])
        pTs = sb("pTs", [P, 2, 8, P])
        yTs = sb("yTs", [P, 2, CH, P])
        xn1 = sb("xn1", [P, 2, C])
        xn1T = sb("xn1T", [C, S])
        vT = sb("vT", [P, S])
        rem = sb("rem", [P, 2, 2, P])
        parts = sb("parts", [P, 2, 3, 2, P], BF16)
        kst = sb("kst", [ROWS, 3, H1, QUART], BF16)
        fT = sb("fT", [P, 6, NS * H1])
        frep = sb("frep", [P, P])
        lnm = sb("lnm", [P, T, NS * H1])
        lz = sb("lz", [P, T, NS * H1])
        optT = sb("optT", [P, P])

        wq_nat = pTs[:].rearrange("p a b c -> p (a b) c")[:, 0:CH, :]
        wq_s = pTs[:].rearrange("p a b c -> p (a b) c")[:, CH:2 * CH, :]
        wo_nat = yTs[:, 0].rearrange("p a (r d) -> p a r d", r=2)
        w_nat = xn1T[:, 0:4 * C].rearrange("p (a c) -> p a c", a=4)
        xn2 = sp[:, 0]
        prod = yTs[:, 1]
        xsc = sp[:, 1].rearrange("p (u t k) c -> p u t k c", u=2, k=2)
        kst3 = xqf[:].rearrange("p a b -> p (a b)").bitcast(BF16).rearrange("p (h n) -> p h n", h=H1)
        qst = xnT[:, 0:S].bitcast(BF16).rearrange("p (h n) -> p h n", n=P)[:, 0:H1, :]
        w1e = xkT[:, 0:FF]
        w2e = xkT[:, FF:2 * FF].rearrange("p (f c) -> p f c", f=FC)
        hT = xkT[:, 2 * FF:3 * FF].rearrange("p (f c) -> p f c", f=FC)

        scr_k = nc.dram_tensor("scr_k", [3, P, S], BF16, kind="Internal").ap()
        scr_q = nc.dram_tensor("scr_q", [len(PAIRS), P, S], BF16, kind="Internal").ap()

        x_in = [sem(f"x_in{c}") for c in range(NQ)]
        wa_in, wb_in, bias_in = sem("wa_in"), sem("wb_in"), sem("bias_in")
        consts = sem("consts")
        dve_pro, pool_pro, act_pro, pe_pro = sem("dve_pro"), sem("pool_pro"), sem("act_pro"), sem("pe_pro")
        nmean2_ready = sem("nmean2_ready")
        xn_ready, xn2_ready, xnT_done, xn_copied, xfT_done, xf_copied = (
            sem("xn_ready"), sem("xn2_ready"), sem("xnT_done"), sem("xn_copied"), sem("xfT_done"), sem("xf_copied"))
        gx_done, ms_ready, ms_eps, rms_ready, xsc_ready, xscT_done, xqk_ready, binT_ready = (
            sem("gx_done"), sem("ms_ready"), sem("ms_eps"), sem("rms_ready"), sem("xsc_ready"), sem("xscT_done"),
            sem("xqk_ready"), sem("binT_ready"))
        amax_ready, gmax_ready, fsc_ready, wabs_ready, tern_step, wqk_scaled, first_masked = (
            sem("amax_ready"), sem("gmax_ready"), sem("fsc_ready"), sem("wabs_ready"), sem("tern_step"),
            sem("wqk_scaled"), sem("first_masked"))
        win_ready, ffx_ready = sem("win_ready"), sem("ffx_ready")
        q_done, kv_done = sem("q_done"), sem("kv_done")
        q_copied, v_copied, k_copied = sem("q_copied"), sem("v_copied"), sem("k_copied")
        scores_done, bias_added, nmax_ready, exp_done = (
            sem("scores_done"), sem("bias_added"), sem("nmax_ready"), sem("exp_done"))
        rz_ready, probs_ready = sem("rz_ready"), sem("probs_ready")
        pT_done, pTa_copied, pTd_copied = sem("pT_done"), sem("pTa_copied"), sem("pTd_copied")
        y_done, ya_copied, yd_copied = sem("y_done"), sem("ya_copied"), sem("yd_copied")
        x1_done, x1_ready, st_ready, mv_ready, rstd_ready, xn1_ready = (
            sem("x1_done"), sem("x1_ready"), sem("st_ready"), sem("mv_ready"), sem("rstd_ready"), sem("xn1_ready"))
        xT_done, xn1T_copied, qkv_done = sem("xT_done"), sem("xn1T_copied"), sem("qkv_done")
        p1_ready, rem_ready, p2_ready, split_ready = (
            sem("p1_ready"), sem("rem_ready"), sem("p2_ready"), sem("split_ready"))
        scr_w = [sem("scr_w0"), sem("scr_w1")]
        kst_in = {0: sem("kst_in0"), 3: sem("kst_in3")}
        ffx_step = sem("ffx_step")
        gate_step, gate_pe, exp_in = sem("gate_step"), sem("gate_pe"), sem("exp_in")
        q_in = [sem("q_in0"), sem("q_in1")]
        l_scores, l_max, l_slots = sem("l_scores"), sem("l_max"), sem("l_slots")
        mn_ready, h_ready = sem("mn_ready"), sem("h_ready")
        biased, ffn_done, ffn_added = sem("biased"), sem("ffn_done"), sem("ffn_added")
        h_done, comb, comb_e, f_done, opt_ready, o_done, o_ready, stored = (
            sem("h_done"), sem("comb"), sem("comb_e"), sem("f_done"), sem("opt_ready"), sem("o_done"),
            sem("o_ready"), sem("stored"))

        block = ctx.enter_context(nc.Block())

        def tiles(eng, step, lag):
            for t in range(4):
                step(t, t % 2)
            with eng.Fori(2, T // 2) as i:
                for u in (0, 1):
                    step(i * 2 + u, u)
            for t in range(T, T + lag):
                step(t, t % 2)

        def has(t, lag=0):
            return not isinstance(t, int) or 0 <= t - lag < T

        def later(t, n=0):
            return not isinstance(t, int) or t - n > 0

        def tok(t):
            return bass.ds(t * P, P)

        NWA, NWB = 13, 11

        @block.sync
        def _(sp_):
            xv = x.rearrange("a (c t p) d -> (a c) p t d", c=NQ, p=P)
            r_of = lambda r: slice(r * HD, (r + 1) * HD)
            wqv = wq.rearrange("(cph r j d) c -> r d cph j c", cph=2, r=2, j=4)
            wov = wo.rearrange("o (cph r j d) -> o cph r j d", cph=2, r=2, j=4)
            qnv = q_norm_w.rearrange("(cph r j d) -> cph r j d", cph=2, r=2, j=4)

            def load_x(c):
                sp_.dma_start(xs[:, c * TQ:(c + 1) * TQ, :], xv[c]).then_inc(x_in[c], 16)

            load_x(0)
            for cph in (0, 1):
                for r in (0, 1):
                    sp_.dma_start(wq_nat[r_of(r), cph * 4:cph * 4 + 4, :], wqv[r, :, cph]).then_inc(wa_in, 16)
            sp_.dma_start(w_kv[:, 0:2, :], wk.rearrange("(a p) c -> p a c", p=P)).then_inc(wa_in, 16)
            sp_.dma_start(w_kv[:, 2:4, :], wv.rearrange("(a p) c -> p a c", p=P)).then_inc(wa_in, 16)
            for cph in (0, 1):
                for r in (0, 1):
                    sp_.dma_start(rows[cph * 4:cph * 4 + 4, r_of(r)], qnv[cph, r]).then_inc(wa_in, 16)
            sp_.dma_start(rows[8:10, :], k_norm_w.rearrange("(a p) -> a p", p=P)).then_inc(wa_in, 16)
            sp_.dma_start(rows[10:11, :], ln_gamma.unsqueeze(0)).then_inc(wa_in, 16)
            sp_.dma_start(rows[11:12, :], ln_beta.unsqueeze(0)).then_inc(wa_in, 16)
            for c in range(1, NQ):
                load_x(c)
            for cph in (0, 1):
                for r in (0, 1):
                    sp_.dma_start(wo_nat[:, cph * 4:cph * 4 + 4, r, :], wov[:, cph, r]).then_inc(wb_in, 16)
            sp_.dma_start(w_nat[:, 0:3, :], w_in.rearrange("(a p) c -> p a c", p=P)).then_inc(wb_in, 16)
            sp_.dma_start(w_nat[:, 3, :], w_out).then_inc(wb_in, 16)
            sp_.dma_start(tern[:], ffn_w).then_inc(wb_in, 16)
            sp_.dma_start(bin_nat[:], b_in.unsqueeze(0)).then_inc(wb_in, 16)
            sp_.dma_start(outb[:, 0, :], b_out.unsqueeze(0).broadcast_to([P, C])).then_inc(wb_in, 16)
            sp_.dma_start(wr_s[:], Wr).then_inc(wb_in, 16)
            sp_.dma_start(br_s[:], br.unsqueeze(0)).then_inc(wb_in, 16)
            sp_.dma_start(biasm[:], alibi).then_inc(bias_in, 16)

            def write_parts(t, u):
                sp_.wait_ge(split_ready, t + 1)
                sp_.dma_start(scr_k[:, :, tok(t)].rearrange("j p n -> p j n"),
                              parts[:, u, :, 1, :]).then_inc(scr_w[u], 16)
                for i, (a, n) in enumerate(((0, 3), (3, 2), (5, 1))):
                    sp_.dma_start(scr_q[a:a + n, :, tok(t)].rearrange("j p n -> p j n"),
                                  parts[:, u, i:i + 1, 0, :].broadcast_to([P, n, P])).then_inc(scr_w[u], 16)

            def read_keys(q, dst, signal):
                for u in (0, 1):
                    sp_.wait_ge(scr_w[u], (q * (TQ // 2) + TQ // 2) * 64)
                src = scr_k.rearrange("j (d h) n -> (j d) h n", h=H1)
                for a, n in ((0, 3), (3, 2), (5, 1)):
                    sp_.dma_start(dst[a * D1:(a + n) * D1], src[0:n * D1, :, bass.ds(q * QUART, QUART)]
                                  ).then_inc(signal, 16)

            with sp_.Fori(0, NQ - 1) as q:
                for j in range(TQ):
                    write_parts(q * TQ + j, j % 2)
                read_keys(q, kst[:, bass.ds(q, 1)].rearrange("p a h n -> p (a h) n"), kst_in[0])
            write_parts(T - 4, 0)

            qsrc = scr_q.rearrange("j (d h) n -> (j d) h n", h=H1)
            sp_.wait_ge(win_ready, T)

            def read_q(t, g):
                hs = slice(g * 8, g * 8 + 8)
                sp_.dma_start(qst[0:ROWS, hs, :], qsrc[:, hs, tok(t)]).then_inc(q_in[g], 16)

            sp_.wait_ge(scr_w[0], (T // 2 - 1) * 64)
            read_q(0, 0)
            read_q(0, 1)
            write_parts(T - 3, 1)
            write_parts(T - 2, 0)
            sp_.wait_ge(kv_done, T)
            sp_.wait_ge(gate_step, 4)
            e = sp_.value_load(gidx[0:1, 0:1], min_val=0, max_val=EXPERTS - 1)
            sp_.dma_start(w1e, W1[bass.ds(e, 1)].rearrange("e c f -> (e c) f")).then_inc(exp_in, 16)
            sp_.dma_start(c1T[:], b1[bass.ds(e, 1), :].rearrange("e (p f) -> p (e f)", f=FC)).then_inc(exp_in, 16)
            write_parts(T - 1, 1)
            sp_.dma_start(w2e, W2[bass.ds(e, 1)].rearrange("e (p f) c -> p (e f) c", f=FC)).then_inc(exp_in, 16)
            sp_.dma_start(outb[:, 1, :], b2[bass.ds(e, 1), :].broadcast_to([P, C])).then_inc(exp_in, 16)
            sp_.wait_ge(q_done, T)
            sp_.wait_ge(ffx_ready, T)
            read_keys(NQ - 1, kst3[0:ROWS], kst_in[3])
            ov = out.rearrange("a (t p) d -> (a t) p d", p=P)
            with sp_.Fori(1, T) as t:
                sp_.wait_ge(l_scores, t * NC - H1 // 2)
                read_q(t, 0)
                sp_.wait_ge(l_scores, t * NC)
                read_q(t, 1)
                sp_.wait_ge(o_ready, t)
                sp_.dma_start(ov[bass.ds(t - 1, 1)].rearrange("a p d -> p (a d)"),
                              x1[:, bass.ds(t - 1, 1), :].rearrange("p a d -> p (a d)")).then_inc(stored, 16)
            sp_.wait_ge(o_ready, T)
            sp_.dma_start(ov[T - 1], x1[:, T - 1, :]).then_inc(stored, 16)
            sp_.wait_ge(stored, 16 * T)

        @block.gpsimd
        def _(pool):
            pool.memset(ident[:], 0.0).then_inc(consts, 1)
            pool.memset(ones[:], 1.0).then_inc(consts, 1)
            pool.memset(cst[:, 0:1], -0.5).then_inc(consts, 1)
            pool.memset(cst[:, 1:2], -1.0).then_inc(consts, 1)
            pool.memset(cst[:, 2:3], 1e-6).then_inc(consts, 1)
            pool.memset(cst[:, 3:4], 0.0).then_inc(consts, 1)
            pool.wait_ge(consts, 6)
            pool.affine_select(out=ident[:], in_=ident[:], compare_op=ALU.not_equal, fill=1.0, base=0,
                               pattern=[[-1, P]], channel_multiplier=1).then_inc(consts, 1)
            pool.memset(ks[:, 0, :, 0, BLK:P], 0.0).then_inc(consts, 1)
            pool.memset(vs[:, 0, 0, :], 0.0).then_inc(consts, 1)
            pool.wait_ge(consts, 9)

            def power(o, i, col, n):
                return pool.tensor_tensor(o, i, cst[:, col:col + 1].broadcast_to([P, n]), ALU.pow)

            quarter = lambda a, c: a[:, c * TQ:(c + 1) * TQ]

            def rstd_a(c):
                pool.wait_ge(dve_pro, 16 * c + 8)
                power(quarter(rstd, c), mv[:, c * TQ:(c + 1) * TQ, 1], 0, TQ).then_inc(pool_pro, 1)

            def rstd_b(c):
                pool.wait_ge(dve_pro, 16 * c + 16)
                power(quarter(rstd2, c), mv2[:, c * TQ:(c + 1) * TQ, 1], 0, TQ).then_inc(pool_pro, 1)
                pool.tensor_tensor(quarter(nmean2, c), mv2[:, c * TQ:(c + 1) * TQ, 0],
                                   cst[:, 1:2].broadcast_to([P, TQ]), ALU.mult).then_inc(nmean2_ready, 1)
                pool.wait_ge(nmean2_ready, 2 * c + 1)
                pool.wait_ge(pool_pro, 2 * c + 2)
                pool.tensor_tensor(quarter(nmean2, c), quarter(nmean2, c), quarter(rstd2, c), ALU.mult
                                   ).then_inc(nmean2_ready, 1)

            def rms(c):
                pool.wait_ge(ms_eps, c + 1)
                power(quarter(rqk, c).rearrange("p t k -> p (t k)"), quarter(ms, c).rearrange("p t k -> p (t k)"),
                      0, 2 * TQ).then_inc(rms_ready, 1)

            def window(t, u):
                if isinstance(t, int) and t in (0, TQ):
                    pool.wait_ge(xn_copied, NQ if t else 1)
                if later(t, 1):
                    pool.wait_ge(kv_done, t - 1)
                pool.tensor_tensor(win[:, u, :], xnT[:, tok(t)], cst[:, 3:4].broadcast_to([P, P]),
                                   ALU.add).then_inc(win_ready, 1)

            rstd_a(0)
            rstd_b(0)
            rstd_a(1)
            rstd_b(1)
            rstd_a(2)
            rms(0)
            rstd_b(2)
            rstd_a(3)
            rms(1)
            rstd_b(3)
            window(0, 0)
            rms(2)
            rms(3)

            def step(t, u):
                v = 1 - u
                if has(t, 2):
                    pool.wait_ge(mv_ready, (t - 1) * 2)
                    power(rstd3[:, u:u + 1], mv3[:, u, 1:2], 0, 1).then_inc(rstd_ready, 1)
                if has(t, -1) and (not isinstance(t, int) or t + 1 < T):
                    window(t + 1, v)

                def normalize(h):
                    pool.wait_ge(rz_ready, t * 2 + h + 1)
                    for r in (0, 1):
                        hs = slice(8 * h + 4 * r, 8 * h + 4 * r + 4)
                        pool.tensor_tensor(sp[:, u, hs, :], sp[:, u, hs, :],
                                           z0[:, u, 2, hs].unsqueeze(2).broadcast_to([P, 4, P]),
                                           ALU.mult).then_inc(probs_ready, 1)

                if has(t):
                    normalize(0)
                if has(t, 2):
                    pool.wait_ge(rem_ready, t - 1)
                    pool.tensor_tensor(parts[:, u, 1], rem[:, u], cst[:, 3:4].unsqueeze(2).broadcast_to([P, 2, P]),
                                       ALU.add).then_inc(p2_ready, 1)
                    pool.wait_ge(p2_ready, t - 1)
                    pool.tensor_tensor(parts[:, u, 2], rem[:, u], parts[:, u, 1],
                                       ALU.subtract).then_inc(split_ready, 1)
                if has(t):
                    normalize(1)
                if isinstance(t, int) and t == 0:
                    pool.wait_ge(amax_ready, NQ + 1)
                    pool.partition_all_reduce(fsc[:, 6:7], fsc[:, 5:6], P, RMAX).then_inc(gmax_ready, 1)

            for t in range(4):
                step(t, t % 2)
            with pool.Fori(2, T // 2 - 1) as i:
                for u in (0, 1):
                    step(i * 2 + u, u)
            for t in range(T - 2, T + 2):
                step(t, t % 2)

            def combine(t, last=False):
                m = lnm[:, bass.ds(t, 1), :].rearrange("p a (h s) -> p (a h) s", s=NS)
                z = lz[:, bass.ds(t, 1), :].rearrange("p a (h s) -> p (a h) s", s=NS)
                d, e, w = (fT[:, k, :].rearrange("p (h s) -> p h s", s=NS) for k in range(1, 4))
                n = t * 5
                pool.wait_ge(l_slots, (t + 1) * NC)
                pool.wait_ge(mn_ready, t + 1)
                pool.tensor_tensor(d, fT[:, 0, 0:H1].unsqueeze(2).broadcast_to([P, H1, NS]), m,
                                   ALU.subtract).then_inc(comb, 1)
                pool.wait_ge(comb_e, t + 1)
                pool.tensor_tensor(w, z, e, ALU.mult).then_inc(comb, 1)
                pool.wait_ge(comb, n + 2)
                pool.tensor_tensor(fT[:, 4, 0:H1], w[:, :, 0], w[:, :, 1], ALU.add).then_inc(comb, 1)
                pool.wait_ge(comb, n + 3)
                if not last:
                    power(fT[:, 5, 0:H1], fT[:, 4, 0:H1], 1, H1).then_inc(comb, 1)
                pool.wait_ge(comb, n + 4)
                pool.tensor_tensor(frep[:].rearrange("p (d h) -> p d h", d=D1),
                                   fT[:, 4:5, 0:H1].broadcast_to([P, D1, H1]),
                                   fT[:, 5:6, 0:H1].broadcast_to([P, D1, H1]), ALU.mult).then_inc(comb, 1)

            pool.wait_ge(exp_in, 64)
            pool.tensor_tensor(outb[:, 2, :], outb[:, 0, :], outb[:, 1, :], ALU.add).then_inc(biased, 1)
            pool.wait_ge(biased, 1)
            pool.tensor_tensor(x1[:], x1[:], outb[:, 2:3, :].broadcast_to([P, T, C]), ALU.add).then_inc(biased, 1)

            with pool.Fori(0, T - 1) as t:
                combine(t)
            combine(T - 1, last=True)

        @block.scalar
        def _(act):
            def copy(o, i, signal, **kw):
                return act.activation(o, i, ACT.Identity, **kw).then_inc(signal, 1)

            bank = lambda b, n=1: ps[:, b:b + n, :].rearrange("p b n -> p (b n)")
            def normed(c):
                act.wait_ge(xnT_done, c + 1)
                copy(xnT[:, c * QUART:(c + 1) * QUART], bank(c % 2), xn_copied)

            def ffn_normed(c):
                act.wait_ge(xfT_done, c + 1)
                if c == 0:
                    act.wait_ge(act_pro, 1)
                copy(xfT[:, c * QUART:(c + 1) * QUART], bank(7), xf_copied, scale=rowsT[:, 10:11],
                     bias=rowsT[:, 11:12])

            def over_rms(c):
                act.wait_ge(rms_ready, c + 1)
                if c > 1:
                    act.wait_ge(xscT_done, c - 1)
                for j in range(TQ):
                    for k in (0, 1):
                        t = c * TQ + j
                        last = act.activation(xsc[:, c % 2, j, k], x1[:, t, :], ACT.Identity,
                                              scale=rqk[:, t, k:k + 1])
                last.then_inc(xsc_ready, 1)

            def over_rms_T(c):
                act.wait_ge(xscT_done, c + 1)
                copy(xqT[:, c * QUART:(c + 1) * QUART], bank(4), xqk_ready)
                copy(xkT[:, c * QUART:(c + 1) * QUART], bank(5), xqk_ready)

            def ffn_norm(c):
                act.wait_ge(nmean2_ready, 2 * c + 2)
                if c > 1:
                    act.wait_ge(xfT_done, c - 1)
                for j in range(TQ):
                    t = c * TQ + j
                    last = act.activation(xn2[:, 4 * (c % 2) + j, :], x1[:, t, :], ACT.Identity,
                                          scale=rstd2[:, t:t + 1], bias=nmean2[:, t:t + 1])
                last.then_inc(xn2_ready, 1)

            normed(0)
            ffn_norm(0)
            act.wait_ge(pe_pro, 1)
            copy(rowsT[:], ps[:, 7, 0:12], act_pro)
            act.wait_ge(pe_pro, 2)
            copy(gram[:], ps[:, 6, 0:2 * C].rearrange("p (a c) -> p a c", a=2), act_pro)
            ffn_normed(0)
            normed(1)
            ffn_norm(1)
            act.wait_ge(pe_pro, 3)
            copy(wqT[:].rearrange("p a b -> p (a b)"), bank(4, 2), act_pro, scale=HD ** -0.5)
            act.wait_ge(pe_pro, 4)
            copy(wkvT[:].rearrange("p a b -> p (a b)"), bank(6), act_pro)
            ffn_normed(1)
            normed(2)
            over_rms(0)
            ffn_norm(2)
            normed(3)
            over_rms_T(0)
            ffn_normed(2)
            ffn_norm(3)
            over_rms(1)
            ffn_normed(3)

            def last_weights():
                act.wait_ge(pe_pro, 5)
                copy(woT[:].rearrange("p a b -> p (a b)"), bank(4, 2), act_pro)
                act.wait_ge(pe_pro, 6)
                win_v = ps[:, 6, 0:3 * C].rearrange("p (h s d) -> p s d h", s=3, d=D1)
                act.activation(w_inT[:, 0], win_v[:, 0], ACT.Identity, scale=D1 ** -0.5)
                act.activation(w_inT[:, 1], win_v[:, 1], ACT.Identity)
                act.activation(w_inT[:, 2], win_v[:, 2], ACT.Identity)
                copy(w_outT[:], ps[:, 6, 3 * C:4 * C], act_pro)
                bin_v = bin_nat[:].rearrange("p (h s d) -> p s d h", s=3, d=D1)
                act.activation(bin_row[:, 0], bin_v[:, 0], ACT.Identity, scale=D1 ** -0.5)
                act.activation(bin_row[:, 1], bin_v[:, 1], ACT.Identity)
                copy(bin_row[:, 2], bin_v[:, 2], act_pro)

            def exps(t, u, a, b):
                for s in range(a, b):
                    last = act.activation(sp[:, u, s, :], sp[:, u, s, :], ACT.Exp, bias=z0[:, u, 0, s:s + 1],
                                          accum_out=z0[:, u, 1, s:s + 1])
                return last

            def copy_pT(t, h):
                act.wait_ge(pT_done, t * 2 + h + 1)
                if later(t):
                    act.wait_ge(y_done, t * 2 + h - 1)
                copy(pTs[:, h, 0:4, :].rearrange("p a b -> p (a b)"), bank(4), pTa_copied)

            def exp_half(t, turn, b):
                h, c = turn
                i = h * NS + c
                act.wait_ge(l_max, t * NC + (HALVES.index(turn) + 1))
                col = lambda a: a[:, bass.ds(t, 1), i:i + 1].rearrange("p a b -> p (a b)")
                act.activation(bank(b, 2), bank(b, 2), ACT.Exp, bias=col(lnm), accum_out=col(lz)).then_inc(l_slots, 1)

            def early(t, step_, *ns):
                if isinstance(t, int) and t == step_:
                    for n in ns:
                        exp_half(0, TURNS[n], 2 * (n % 2))

            def step(t, u):
                v = 1 - u
                early(t, T, 0)
                if has(t):
                    act.wait_ge(kv_done, t + 1)
                    if later(t, 1):
                        act.wait_ge(y_done, (t - 1) * 2)
                    act.activation(vs[:, u, 1, :], ps[:, 3, 0:2 * C], ACT.Identity)
                    own = act.activation(vs[0:BLK, u, 0, :], ps[0:BLK, 3, 0:2 * C], ACT.Identity)
                    if later(t):
                        act.wait_ge(v_copied, t)
                        copy(vs[BLK:P, u, 0, :], vs[BLK:P, v, 1, :], v_copied)
                    else:
                        own.then_inc(v_copied, 1)
                if isinstance(t, int) and t == 0:
                    over_rms_T(1)
                    over_rms(2)
                    over_rms(3)
                    over_rms_T(2)
                if has(t, 1):
                    copy_pT(t - 1, 0)
                early(t, T, 1)
                if has(t, 1):
                    act.wait_ge(y_done, (t - 1) * 2 + 1)
                    if later(t - 1, 1):
                        act.wait_ge(x1_done, t - 2)
                    copy(yTs[:, v, 0:4, :].rearrange("p j (b q) -> p b j q", b=2),
                         ps[:, 6, :].rearrange("p (b j q) -> p b j q", b=2, j=4), ya_copied)
                if has(t, 1):
                    copy_pT(t - 1, 1)
                if has(t, 2):
                    act.wait_ge(xT_done, t - 1)
                    act.activation(xn1T[:, tok(t - 2)], ps[:, 7, 0:P], ACT.Identity,
                                   accum_out=xsum[:, bass.ds(t - 2, 1)]).then_inc(xn1T_copied, 1)
                early(t, T, 2)
                early(t, T + 1, 5, 6)
                if has(t):
                    act.wait_ge(nmax_ready, t * 2 + 1)
                    if later(t, 1):
                        act.wait_ge(probs_ready, (t - 1) * 4)
                    exps(t, u, 0, 4)
                if has(t, 2):
                    act.wait_ge(qkv_done, t - 1)
                    if isinstance(t, int) and t == 2:
                        act.wait_ge(binT_ready, 1)
                    act.activation(vT[:, tok(t - 2)], ps[:, 7, 3 * P:4 * P], ACT.Identity, bias=binT[:, 2:3])
                    if later(t - 2, 1):
                        act.wait_ge(scr_w[u], (t - 2 - u) * 32)
                    act.activation(parts[:, u, 0, 0], ps[:, 7, P:2 * P], ACT.Identity, bias=binT[:, 0:1])
                    copy(parts[:, u, 0, 1], ps[:, 7, 2 * P:3 * P], p1_ready, bias=binT[:, 1:2])
                if has(t):
                    exps(t, u, 4, 8).then_inc(exp_done, 1)
                if isinstance(t, int) and t == 0:
                    last_weights()
                    over_rms_T(3)
                if has(t):
                    act.wait_ge(nmax_ready, t * 2 + 2)
                    exps(t, u, 8, 16).then_inc(exp_done, 1)
                early(t, T, 3, 4)
                early(t, T + 1, 7)

            tiles(act, step, 2)

            def combine_exp(t):
                act.wait_ge(comb, t * 5 + 1)
                act.activation(fT[:, 2, :], fT[:, 1, :], ACT.Exp).then_inc(comb_e, 1)

            def hidden(t, g):
                act.wait_ge(h_done, t * 2 + g + 1)
                if later(t):
                    act.wait_ge(ffn_done, t * 2)
                b = 2 * (AT["AB"[g]] % BUFS)
                for n in range(2):
                    f = 2 * g + n
                    last = act.activation(hT[:, f, :], ps[:, b, n * P:(n + 1) * P], ACT.Relu, bias=c1T[:, f:f + 1])
                last.then_inc(h_ready, 1)

            def attend(t, lagged, start=0):
                for p, turn in enumerate(TURNS):
                    if p < start:
                        continue
                    if isinstance(turn, tuple):
                        exp_half(t, turn, 2 * (p % BUFS))
                    if lagged and p == 3:
                        combine_exp(t - 1)
                    if turn in ("A", "B"):
                        hidden(t, "AB".index(turn))

            attend(0, False, EARLY)
            with act.Fori(1, T) as t:
                attend(t, True)
            combine_exp(T - 1)

        @block.vector
        def _(dve):
            bank = lambda b, n=1: ps[:, b:b + n, :].rearrange("p b n -> p (b n)")

            tiles_of = lambda c: range(c * TQ, (c + 1) * TQ)
            quarter = lambda c: slice(c * TQ, (c + 1) * TQ)

            def variance(c, x_, st_, mv_, eps, n):
                for t in tiles_of(c):
                    dve.bn_stats(st_[:, t, :], x_[:, t, :]).then_inc(dve_pro, 1)
                dve.wait_ge(dve_pro, n + 4)
                for t in tiles_of(c):
                    last = dve.bn_aggr(mv_[:, t, :], st_[:, t, :])
                last.then_inc(dve_pro, 3)
                dve.wait_ge(dve_pro, n + 7)
                dve.tensor_scalar(mv_[:, quarter(c), 1], mv_[:, quarter(c), 1], eps, None, ALU.add
                                  ).then_inc(dve_pro, 1)

            def stats(c):
                dve.wait_ge(x_in[c], 16)
                variance(c, xs, st, mv, 1e-5, 16 * c)

            def norm(c):
                dve.wait_ge(pool_pro, 2 * c + 1)
                for t in tiles_of(c):
                    dve.tensor_scalar(x1[:, t, :], xs[:, t, :], mv[:, t, 0:1], rstd[:, t:t + 1], ALU.subtract,
                                      ALU.mult).then_inc(xn_ready, 1)
                dve.wait_ge(xn_ready, 4 * (c + 1))
                variance(c, x1, st2, mv2, 1e-3, 16 * c + 8)

            def mean_squares(c):
                dve.wait_ge(gx_done, c + 1)
                if c:
                    dve.wait_ge(ms_ready, c)
                for j, t in enumerate(tiles_of(c)):
                    for k, n in ((0, HEADS * HD), (1, KV * HD)):
                        last = dve.scalar_tensor_tensor(prod[:, 2 * j + k, :],
                                                        ps[:, 2 + j // 2, (j % 2 * 2 + k) * P:(j % 2 * 2 + k + 1) * P],
                                                        1.0 / n, x1[:, t, :], ALU.mult, ALU.mult,
                                                        accum_out=ms[:, t, k:k + 1])
                last.then_inc(ms_ready, 1)
                dve.wait_ge(ms_ready, c + 1)
                dve.tensor_scalar(ms[:, quarter(c), :].rearrange("p t k -> p (t k)"),
                                  ms[:, quarter(c), :].rearrange("p t k -> p (t k)"), 0.0, 1e-6, ALU.max,
                                  ALU.add).then_inc(ms_eps, 1)

            def ffn_max(c):
                dve.wait_ge(xf_copied, c + 1)
                dve.tensor_reduce(fsc[:, 1 + c:2 + c], xfT[:, c * QUART:(c + 1) * QUART], AX.X, ALU.max,
                                  apply_absolute_value=True).then_inc(amax_ready, 1)

            def ternary():
                dve.wait_ge(pe_pro, 7)
                dve.tensor_scalar(fsc[:, 10:11], ps[:, 6, 0:1], 1.0 / (C * C), None, ALU.mult).then_inc(tern_step, 1)
                dve.wait_ge(pe_pro, 8)
                dve.tensor_copy(binT[:], ps[:, 6, 1:4]).then_inc(binT_ready, 1)
                dve.wait_ge(tern_step, 1)
                dve.tensor_scalar(fsc[:, 11:12], fsc[:, 10:11], 1e-5, None, ALU.add).then_inc(tern_step, 1)
                dve.wait_ge(tern_step, 2)
                dve.reciprocal(fsc[:, 12:13], fsc[:, 11:12]).then_inc(tern_step, 1)
                dve.wait_ge(tern_step, 3)
                dve.tensor_scalar(tern[:], tern[:], fsc[:, 12:13], ROUND, ALU.mult, ALU.add).then_inc(tern_step, 1)
                dve.wait_ge(tern_step, 4)
                dve.tensor_scalar(tern[:], tern[:], ROUND, 1.0, ALU.subtract, ALU.min).then_inc(tern_step, 1)
                dve.wait_ge(tern_step, 5)
                dve.tensor_scalar(tern[:], tern[:], -1.0, None, ALU.max).then_inc(tern_step, 1)

            stats(0)
            norm(0)
            stats(1)
            norm(1)
            stats(2)
            dve.wait_ge(act_pro, 1)
            dve.wait_ge(wa_in, 16 * NWA)
            dve.tensor_tensor(wq_s, wq_nat, rowsT[:, 0:CH].unsqueeze(2).broadcast_to([P, CH, C]),
                              ALU.mult).then_inc(wqk_scaled, 1)
            dve.tensor_tensor(wk_s[:], w_kv[:, 0:2, :], rowsT[:, 8:10].unsqueeze(2).broadcast_to([P, 2, C]),
                              ALU.mult).then_inc(wqk_scaled, 1)
            mean_squares(0)
            norm(2)
            stats(3)
            mean_squares(1)
            norm(3)
            dve.wait_ge(wb_in, 16 * NWB)
            dve.tensor_copy(optT[:].rearrange("p (d h) -> p d h", d=D1),
                            w_nat[:, 3, :].rearrange("p (h d) -> p d h", d=D1)).then_inc(wqk_scaled, 1)
            dve.tensor_reduce(fsc[:, 0:1], tern[:], AX.X, ALU.add, apply_absolute_value=True).then_inc(wabs_ready, 1)
            ffn_max(0)
            mean_squares(2)
            ffn_max(1)
            ffn_max(2)
            mean_squares(3)
            dve.wait_ge(bias_in, 16)

            def ffn_scales():
                dve.wait_ge(gmax_ready, 1)
                dve.reciprocal(fsc[:, 7:8], fsc[:, 6:7]).then_inc(fsc_ready, 1)
                dve.tensor_scalar(fsc[:, 13:14], fsc[:, 6:7], 1.0 / 128.0, None, ALU.mult).then_inc(fsc_ready, 1)
                dve.wait_ge(fsc_ready, 2)
                dve.tensor_scalar(fsc[:, 8:9], fsc[:, 7:8], 128.0, None, ALU.mult).then_inc(fsc_ready, 1)
                dve.tensor_tensor(fsc[:, 9:10], fsc[:, 13:14], fsc[:, 10:11], ALU.mult).then_inc(fsc_ready, 1)
                dve.wait_ge(fsc_ready, 4)

            def ffn_input(t, u):
                if later(t, 1):
                    dve.wait_ge(x1_done, t - 1)
                dve.tensor_scalar(ffx[:, u, 0, :], xfT[:, tok(t)], fsc[:, 8:9], LIM, ALU.mult,
                                  ALU.min).then_inc(ffx_step, 1)
                dve.wait_ge(ffx_step, t + 1)
                dve.tensor_scalar(ffx[:, u, 1, :], ffx[:, u, 0, :], -LIM, fsc[:, 9:10], ALU.max,
                                  ALU.mult).then_inc(ffx_ready, 1)

            def add_bias(t, u, h):
                dve.wait_ge(scores_done, t * 2 + h + 1)
                if later(t, 1):
                    dve.wait_ge(pT_done, (t - 1) * 2)
                for r in (0, 1):
                    s = 8 * h + 4 * r
                    bv = biasm[:, :, 4 * h + 2 * r:4 * h + 2 * r + 2, :].rearrange("p b a n -> p b (a n)")
                    last = dve.tensor_tensor(sp[:, u, s:s + 4, :].rearrange("p (b a) n -> p b (a n)", b=2),
                                             ps[:, 2 * h + r, :].rearrange("p (b n) -> p b n", b=2),
                                             bv, ALU.add)
                last.then_inc(bias_added, 1)
                dve.wait_ge(bias_added, t * 2 + h + 1)
                if isinstance(t, int) and t == 0:
                    for r in (0, 1):
                        s = 8 * h + 4 * r
                        last = dve.memset(sp[:, u, s:s + 2, BLK:P], BIG)
                    last.then_inc(first_masked, 1)

            def row_max(t, u, h):
                if isinstance(t, int) and t == 0:
                    dve.wait_ge(first_masked, h + 1)
                hs = slice(8 * h, 8 * h + 8)
                dve.tensor_reduce(z0[:, u, 0, hs], sp[:, u, hs, :], AX.X, ALU.max,
                                  negate=True).then_inc(nmax_ready, 1)

            def reciprocal(t, u, h):
                hs = slice(8 * h, 8 * h + 8)
                dve.wait_ge(exp_done, t * 2 + h + 1)
                if later(t, 1):
                    dve.wait_ge(probs_ready, (t - 2) * 4 + 2 * h + 2)
                dve.reciprocal(z0[:, u, 2, hs], z0[:, u, 1, hs]).then_inc(rz_ready, 1)

            def copy_pT(t, h):
                dve.wait_ge(pT_done, t * 2 + h + 1)
                if later(t):
                    dve.wait_ge(y_done, t * 2 + h - 1)
                dve.tensor_copy(pTs[:, h, 4:8, :].rearrange("p a b -> p (a b)"), bank(5)).then_inc(pTd_copied, 1)

            def max_half(t, turn, b):
                h, c = turn
                i = h * NS + c
                dve.wait_ge(l_scores, t * NC + (HALVES.index(turn) + 1))
                dve.tensor_reduce(lnm[:, bass.ds(t, 1), i:i + 1].rearrange("p a b -> p (a b)"),
                                  bank(b, 2), AX.X, ALU.max, negate=True).then_inc(l_max, 1)

            def choose_expert():
                dve.wait_ge(xn1T_copied, T)
                dve.tensor_reduce(xsum[:, T:T + 1], xsum[:, 0:T], AX.X, ALU.add).then_inc(gate_step, 1)
                dve.wait_ge(gate_pe, 1)
                dve.scalar_tensor_tensor(gate[:, 0, :], ps[0:1, 6, 0:EXPERTS], 1.0 / S, br_s[:], ALU.mult,
                                         ALU.add).then_inc(gate_step, 1)
                dve.wait_ge(gate_step, 2)
                dve.max(gate[:, 1, :], gate[:, 0, :]).then_inc(gate_step, 1)
                dve.wait_ge(gate_step, 3)
                dve.max_index(gidx[:], gate[:, 1, :], gate[:, 0, :]).then_inc(gate_step, 1)

            def early(t, step_, *ns):
                if isinstance(t, int) and t == step_:
                    for n in ns:
                        max_half(0, TURNS[n], 2 * (n % 2))

            def step(t, u):
                v = 1 - u
                early(t, T, 0, 1)
                if has(t):
                    dve.wait_ge(q_done, t + 1)
                    if later(t, 1):
                        dve.wait_ge(scores_done, (t - 1) * 2)
                    dve.tensor_copy(qs[:, u].rearrange("p a b -> p (a b)"), bank(0, 2)).then_inc(q_copied, 1)
                    dve.wait_ge(kv_done, t + 1)
                    kv = ps[:, 2, 0:2 * P].rearrange("p (j n) -> p j n", j=2)
                    dve.tensor_copy(ks[:, u, :, 1, :], kv)
                    own = dve.tensor_copy(ks[:, u, :, 0, 0:BLK], kv[:, :, 0:BLK])
                    if later(t):
                        dve.wait_ge(k_copied, t)
                        dve.tensor_copy(ks[:, u, :, 0, BLK:P], ks[:, v, :, 1, BLK:P]).then_inc(k_copied, 1)
                    else:
                        own.then_inc(k_copied, 1)
                if has(t, 1) and not (isinstance(t, int) and t == 1):
                    ffn_input(t - 1, v)
                if has(t, 1):
                    reciprocal(t - 1, v, 1)
                if has(t, 2):
                    dve.wait_ge(x1_done, t - 1)
                    dve.tensor_tensor(x1[:, bass.ds(t - 2, 1), :].rearrange("p a c -> p (a c)"),
                                      xs[:, bass.ds(t - 2, 1), :].rearrange("p a c -> p (a c)"),
                                      ps[:, 7, 0:C], ALU.add).then_inc(x1_ready, 1)
                if has(t, 1):
                    copy_pT(t - 1, 0)
                if has(t, 2):
                    dve.wait_ge(bias_in, 16)
                    dve.wait_ge(x1_ready, t - 1)
                    dve.bn_stats(st3[:, u, :], x1[:, bass.ds(t - 2, 1), :].rearrange("p a c -> p (a c)")).then_inc(st_ready, 1)
                    dve.wait_ge(bias_in, 16)
                    dve.wait_ge(st_ready, t - 1)
                    dve.bn_aggr(mv3[:, u, :], st3[:, u, :]).then_inc(mv_ready, 1)
                    dve.wait_ge(mv_ready, (t - 2) * 2 + 1)
                    dve.tensor_scalar(mv3[:, u, 1:2], mv3[:, u, 1:2], 1e-5, None, ALU.add).then_inc(mv_ready, 1)
                if isinstance(t, int) and t == 1:
                    ternary()
                early(t, T, 2)
                early(t, T + 1, 5)
                if has(t):
                    add_bias(t, u, 0)
                if has(t, 2):
                    dve.wait_ge(rstd_ready, t - 1)
                    if later(t - 2, 1):
                        dve.wait_ge(xT_done, t - 3)
                    dve.tensor_scalar(xn1[:, u, :], x1[:, bass.ds(t - 2, 1), :].rearrange("p a c -> p (a c)"), mv3[:, u, 0:1],
                                      rstd3[:, u:u + 1], ALU.subtract, ALU.mult).then_inc(xn1_ready, 1)
                early(t, T + 1, 6)
                if isinstance(t, int) and t == T + 1:
                    choose_expert()
                if has(t, 1):
                    copy_pT(t - 1, 1)
                early(t, T, 3)
                if has(t):
                    row_max(t, u, 0)
                    add_bias(t, u, 1)
                if has(t, 1):
                    dve.wait_ge(y_done, t * 2)
                    if later(t - 1, 1):
                        dve.wait_ge(x1_done, t - 2)
                    dve.tensor_copy(yTs[:, v, 4:8, :].rearrange("p j (b q) -> p b j q", b=2),
                                    ps[:, 6, :].rearrange("p (b j q) -> p b j q", b=2, j=4)).then_inc(yd_copied, 1)
                if has(t):
                    row_max(t, u, 1)
                if isinstance(t, int) and t == 0:
                    ffn_max(3)
                    dve.wait_ge(amax_ready, NQ)
                    dve.tensor_reduce(fsc[:, 5:6], fsc[:, 1:5], AX.X, ALU.max).then_inc(amax_ready, 1)
                if isinstance(t, int) and t == 1:
                    ffn_scales()
                    ffn_input(0, 0)
                early(t, T, 4)
                early(t, T + 1, 7)
                if has(t, 2):
                    dve.wait_ge(p1_ready, t - 1)
                    if later(t - 2, 1):
                        dve.wait_ge(split_ready, t - 3)
                    for i in (0, 1):
                        last = dve.scalar_tensor_tensor(rem[:, u, i], ps[:, 7, (i + 1) * P:(i + 2) * P],
                                                        binT[:, i:i + 1], parts[:, u, 0, i], ALU.add, ALU.subtract)
                    last.then_inc(rem_ready, 1)
                if has(t):
                    reciprocal(t, u, 0)

            tiles(dve, step, 2)

            def row_maxima(t):
                dve.wait_ge(l_max, (t + 1) * NC)
                if later(t):
                    dve.wait_ge(comb, t * 5)
                dve.tensor_reduce(fT[:, 0, 0:H1], lnm[:, bass.ds(t, 1), :].rearrange("p a (h s) -> p (a h) s", s=NS),
                                  AX.X, ALU.min).then_inc(mn_ready, 1)

            def weigh(t):
                dve.wait_ge(f_done, t + 1)
                if later(t):
                    dve.wait_ge(o_done, t)
                dve.tensor_tensor(optT[:], vT[:, tok(t)], ps[:, 2 * (AT["A"] % BUFS) + 1, 0:P], ALU.mult
                                  ).then_inc(opt_ready, 1)

            def finish(t):
                dve.wait_ge(o_done, t + 1)
                dve.wait_ge(ffn_added, (t + 1) * 2)
                xv = x1[:, bass.ds(t, 1), :].rearrange("p a c -> p (a c)")
                dve.tensor_tensor(xv, xv, ps[:, 2 * (AT["B"] % BUFS) + 1, 0:C], ALU.add).then_inc(o_ready, 1)

            def add_ffn(t, g):
                dve.wait_ge(ffn_done, t * 2 + g + 1)
                if g:
                    dve.wait_ge(ffn_added, t * 2 + 1)
                elif not later(t):
                    dve.wait_ge(biased, 2)
                xv = x1[:, bass.ds(t, 1), :].rearrange("p a c -> p (a c)")
                dve.tensor_tensor(xv, xv, ps[:, 2 * (AT["CD"[g]] % BUFS), 0:C], ALU.add).then_inc(ffn_added, 1)

            def maxima(t, lagged, start=0):
                for p, turn in enumerate(TURNS):
                    if p < start:
                        continue
                    if isinstance(turn, tuple):
                        max_half(t, turn, 2 * (p % BUFS))
                    if lagged and p == 1:
                        row_maxima(t - 1)
                    if lagged and turn == "A":
                        weigh(t - 1)
                    if lagged and turn == "B":
                        finish(t - 1)
                    if turn in ("C", "D"):
                        add_ffn(t, "CD".index(turn))

            maxima(0, False, EARLY)
            with dve.Fori(1, T) as t:
                maxima(t, True)
            row_maxima(T - 1)
            dve.wait_ge(comb, (T - 1) * 5 + 3)
            dve.reciprocal(fT[:, 5, 0:H1], fT[:, 4, 0:H1]).then_inc(comb, 1)
            weigh(T - 1)
            finish(T - 1)

        @block.tensor
        def _(pe):
            def normed(c):
                pe.wait_ge(xn_ready, 4 * (c + 1))
                if c > 1:
                    pe.wait_ge(xn_copied, c - 1)
                for j in range(TQ):
                    last = pe.transpose(ps[:, c % 2, j * P:(j + 1) * P], x1[:, c * TQ + j, :], ident[:])
                last.then_inc(xnT_done, 1)

            def ffn_normed(c):
                pe.wait_ge(xn2_ready, c + 1)
                if c:
                    pe.wait_ge(xf_copied, c)
                else:
                    pe.wait_ge(act_pro, 1)
                for j in range(TQ):
                    last = pe.transpose(ps[:, 7, j * P:(j + 1) * P], xn2[:, 4 * (c % 2) + j, :], ident[:])
                last.then_inc(xfT_done, 1)

            def gram_x(c):
                pe.wait_ge(xn_copied, c + 1)
                if c:
                    pe.wait_ge(ms_ready, c)
                else:
                    pe.wait_ge(act_pro, 2)
                for j in range(TQ):
                    last = pe.matmul(ps[:, 2 + j // 2, j % 2 * 2 * P:(j % 2 + 1) * 2 * P],
                                     xnT[:, (c * TQ + j) * P:(c * TQ + j + 1) * P],
                                     gram[:].rearrange("p k c -> p (k c)"), start=True, stop=True)
                last.then_inc(gx_done, 1)

            def over_rms(c):
                pe.wait_ge(xsc_ready, c + 1)
                if c:
                    pe.wait_ge(xqk_ready, 2 * c)
                if c == NQ - 1:
                    pe.wait_ge(act_pro, 5)
                for k in (0, 1):
                    for j in range(TQ):
                        last = pe.transpose(ps[:, 4 + k, j * P:(j + 1) * P], xsc[:, c % 2, j, k], ident[:])
                last.then_inc(xscT_done, 1)

            pe.wait_ge(consts, 9)
            normed(0)
            pe.wait_ge(wa_in, 16 * NWA)
            pe.transpose(ps[:, 7, 0:12], rows[:], ident[0:12, 0:12]).then_inc(pe_pro, 1)
            for j in range(CH):
                pe.matmul(ps[:, 6, 0:C], wq_nat[:, j, :], wq_nat[:, j, :], start=(j == 0), stop=(j == CH - 1))
            for j in range(2):
                last = pe.matmul(ps[:, 6, C:2 * C], w_kv[:, j, :], w_kv[:, j, :], start=(j == 0), stop=(j == 1))
            last.then_inc(pe_pro, 1)
            gram_x(0)
            ffn_normed(0)
            normed(1)
            pe.wait_ge(wqk_scaled, 2)
            for j in range(CH):
                last = pe.transpose(ps[:, 4 + j // 4, (j % 4) * P:(j % 4 + 1) * P], wq_s[:, j, :], ident[:])
            last.then_inc(pe_pro, 1)
            for j in range(2):
                pe.transpose(ps[:, 6, j * P:(j + 1) * P], wk_s[:, j, :], ident[:])
            for j in range(2, 4):
                last = pe.transpose(ps[:, 6, j * P:(j + 1) * P], w_kv[:, j, :], ident[:])
            last.then_inc(pe_pro, 1)
            gram_x(1)
            ffn_normed(1)
            normed(2)
            pe.wait_ge(act_pro, 3)
            gram_x(2)
            normed(3)
            over_rms(0)
            ffn_normed(2)
            gram_x(3)
            ffn_normed(3)

            def last_weights():
                pe.wait_ge(wb_in, 16 * NWB)
                pe.wait_ge(xqk_ready, 6)
                for j in range(CH):
                    last = pe.transpose(ps[:, 4 + j // 4, (j % 4) * P:(j % 4 + 1) * P], wo_nat[:, j].rearrange("p r d -> p (r d)"), ident[:])
                last.then_inc(pe_pro, 1)
                pe.wait_ge(wqk_scaled, 3)
                pe.wait_ge(act_pro, 4)
                for j in range(4):
                    last = pe.transpose(ps[:, 6, j * P:(j + 1) * P],
                                        w_nat[:, j, :] if j < 3 else optT[:],
                                        ident[:])
                last.then_inc(pe_pro, 1)

            def sums_to_partitions():
                pe.wait_ge(act_pro, 7)
                pe.wait_ge(wabs_ready, 1)
                pe.matmul(ps[:, 6, 0:1], ones[:], fsc[:, 0:1], start=True, stop=True).then_inc(pe_pro, 1)
                for i in range(3):
                    last = pe.matmul(ps[:, 6, 1 + i:2 + i], bin_row[:, i].rearrange("p d h -> p (d h)"),
                                     ones[0:1, 0:1], start=True, stop=True)
                last.then_inc(pe_pro, 1)

            def project(t, u):
                pe.wait_ge(win_ready, t + 1)
                if later(t):
                    pe.wait_ge(bias_added, t * 2)
                qv = ps[:, 0:2, :].rearrange("p c (g b a q) -> p c g a b q", g=2, b=2, a=2)
                for j in range(CH):
                    last = pe.matmul(qv[:, j // 4, j % 4 // 2, j % 2], wqT[:, j, :], xqT[:, tok(t)],
                                     start=True, stop=True)
                last.then_inc(q_done, 1)
                for j in range(2):
                    pe.matmul(ps[:, 2, j * P:(j + 1) * P], wkvT[:, j, :], xkT[:, tok(t)], start=True, stop=True)
                last = pe.matmul(ps[:, 3, 0:2 * C], win[:, u, :], wkvT[:, 2:4, :].rearrange("p a b -> p (a b)"),
                                 start=True, stop=True)
                last.then_inc(kv_done, 1)

            def scores(t, u, h):
                pe.wait_ge(q_copied, t + 1)
                pe.wait_ge(k_copied, t + 1)
                if h:
                    pe.wait_ge(v_copied, t + 1)
                for b in range(2):
                    for a in range(2):
                        for r in range(2):
                            rr = slice(r * HD, (r + 1) * HD)
                            last = pe.matmul(ps[:, 2 * h + r, (2 * b + a) * P:(2 * b + a + 1) * P],
                                             qs[rr, u, 4 * h + 2 * a + b, :],
                                             ks[rr, u, h, b, :], start=True, stop=True)
                last.then_inc(scores_done, 1)

            def transpose_probs(t, u, h):
                for r in (0, 1):
                    pe.wait_ge(probs_ready, t * 4 + 2 * h + r + 1)
                    if r == 0 and (later(t) or h):
                        pe.wait_ge(pTa_copied, t * 2 + h)
                        pe.wait_ge(pTd_copied, t * 2 + h)
                    for s in range(4):
                        last = pe.transpose(ps[:, 4 + r, s * P:(s + 1) * P], sp[:, u, 8 * h + 4 * r + s, :], ident[:])
                last.then_inc(pT_done, 1)

            def values(t, u, h):
                pe.wait_ge(pTa_copied, t * 2 + h + 1)
                pe.wait_ge(pTd_copied, t * 2 + h + 1)
                if h:
                    pe.wait_ge(ya_copied, t + 1)
                elif later(t):
                    pe.wait_ge(yd_copied, t)
                else:
                    pe.wait_ge(tern_step, 1)
                    pe.wait_ge(binT_ready, 1)
                for b in range(2):
                    for r in range(2):
                        g = 2 * h + r
                        last = pe.matmul(ps[r * HD:(r + 1) * HD, 6, b * 256:(b + 1) * 256],
                                         vs[:, u, b, g * HD:(g + 1) * HD],
                                         pTs[:, h, 4 * r + 2 * b:4 * r + 2 * b + 2, :].rearrange("p a b -> p (a b)"),
                                         start=True, stop=True)
                last.then_inc(y_done, 1)

            def project_out(t, u):
                pe.wait_ge(ya_copied, t + 1)
                pe.wait_ge(yd_copied, t + 1)
                pe.wait_ge(ffx_ready, t + 1)
                if later(t):
                    pe.wait_ge(rem_ready, t)
                elif isinstance(t, int):
                    pe.wait_ge(tern_step, 6)
                for j in range(CH):
                    pe.matmul(ps[:, 7, 0:C], yTs[:, u, j, :], woT[:, j, :], start=(j == 0), stop=False)
                pe.matmul(ps[:, 7, 0:C], ffx[:, u, 1, :], tern[:], start=False, stop=True).then_inc(x1_done, 1)

            def score_half(turn, b):
                h, c = turn
                for n in range(2):
                    q = 2 * c + n
                    rhs = kst[:, q, h, :] if q < 3 else kst3[0:ROWS, h, :]
                    last = pe.matmul(ps[:, b + n, :], qst[0:ROWS, h, :], rhs, start=True, stop=True)
                last.then_inc(l_scores, 1)

            def early(t, step_, *ns):
                if isinstance(t, int) and t == step_:
                    for n in ns:
                        if n == 0:
                            pe.wait_ge(bias_added, 2 * T)
                            pe.wait_ge(q_in[0], 16)
                            pe.wait_ge(kst_in[0], 16 * 3 * (NQ - 1))
                        if n >= 2:
                            pe.wait_ge(l_slots, n - 1)
                        score_half(TURNS[n], 2 * (n % 2))

            def step(t, u):
                v = 1 - u
                early(t, T, 0, 1)
                if has(t):
                    if isinstance(t, int) and t == 0:
                        pe.wait_ge(xqk_ready, 2)
                        pe.wait_ge(act_pro, 4)
                        pe.wait_ge(ms_ready, NQ)
                    project(t, u)
                    if isinstance(t, int) and t == 0:
                        over_rms(1)
                    if isinstance(t, int) and t == 1:
                        over_rms(NQ - 1)
                        sums_to_partitions()
                if has(t, 2):
                    project_out(t - 2, u)
                if isinstance(t, int) and t == 1:
                    pe.wait_ge(xqk_ready, 2 * NQ)
                    pe.wait_ge(xf_copied, NQ)
                early(t, T + 1, 5, 6)
                if has(t, 1):
                    transpose_probs(t - 1, v, 0)
                early(t, T, 2)
                if has(t):
                    scores(t, u, 0)
                if has(t, 1):
                    values(t - 1, v, 0)
                early(t, T, 3)
                if has(t, 1):
                    transpose_probs(t - 1, v, 1)
                if has(t):
                    scores(t, u, 1)
                if has(t, 2):
                    pe.wait_ge(xn1_ready, t - 1)
                    pe.transpose(ps[:, 7, 0:P], xn1[:, u, :], ident[:]).then_inc(xT_done, 1)
                if has(t, 1):
                    values(t - 1, v, 1)
                if has(t, 2):
                    pe.wait_ge(xn1T_copied, t - 1)
                    for s in range(3):
                        o = ps[:, 7, (s + 1) * P:(s + 2) * P]
                        last = pe.matmul(o, w_inT[:, s].rearrange("p d h -> p (d h)"), xn1T[:, tok(t - 2)],
                                         start=True, stop=True)
                    last.then_inc(qkv_done, 1)
                early(t, T, 4)
                if isinstance(t, int) and t == T + 1:
                    pe.wait_ge(gate_step, 1)
                    pe.matmul(ps[0:1, 6, 0:EXPERTS], xsum[:, T:T + 1], wr_s[:], start=True, stop=True
                              ).then_inc(gate_pe, 1)
                early(t, T + 1, 7)
                if isinstance(t, int) and t == 0:
                    over_rms(2)
                    last_weights()

            tiles(pe, step, 2)


            def replicate(t):
                pe.wait_ge(comb, t * 5 + 5)
                pe.transpose(ps[:, 2 * (AT["A"] % BUFS) + 1, 0:P], frep[:], ident[:]).then_inc(f_done, 1)

            def attn_out(t):
                pe.wait_ge(opt_ready, t + 1)
                pe.matmul(ps[:, 2 * (AT["B"] % BUFS) + 1, 0:C], optT[:], w_outT[:], start=True, stop=True
                          ).then_inc(o_done, 1)

            def hidden(t, g):
                for n in range(2):
                    f = 2 * g + n
                    last = pe.matmul(ps[:, 2 * (AT["AB"[g]] % BUFS), n * P:(n + 1) * P], w1e[:, f:FF:FC],
                                     xn1T[:, tok(t)], start=True, stop=True)
                last.then_inc(h_done, 1)

            def expert_out(t, g):
                pe.wait_ge(h_ready, t * 2 + g + 1)
                for n in range(2):
                    f = 2 * g + n
                    last = pe.matmul(ps[:, 2 * (AT["CD"[g]] % BUFS), 0:C], hT[:, f, :], w2e[:, f, :],
                                     start=(n == 0), stop=(n == 1))
                last.then_inc(ffn_done, 1)

            def wait_free(p, t, first, lagged):
                q, s, lg = p - BUFS, t, lagged
                if first and q < EARLY:
                    if p % BUFS < 2:
                        pe.wait_ge(l_slots, EARLY - 1 + p % BUFS)
                    else:
                        pe.wait_ge(pTa_copied, 2 * T)
                        pe.wait_ge(pTd_copied, 2 * T)
                        pe.wait_ge(gate_step, 2)
                        pe.wait_ge(rem_ready, T)
                    return
                if q < 0:
                    q, s, lg = q + len(TURNS), t - 1, True
                user = TURNS[q]
                if isinstance(user, tuple):
                    pe.wait_ge(l_slots, s * NC + (HALVES.index(user) + 1))
                elif user in "CD":
                    pe.wait_ge(ffn_added, s * 2 + (1 + "CD".index(user)))
                else:
                    pe.wait_ge(h_ready, s * 2 + (1 + "AB".index(user)))
                    if lg:
                        pe.wait_ge(opt_ready if user == "A" else o_ready, s)

            def attend(t, first, lagged):
                for p, turn in enumerate(TURNS):
                    if first and p < EARLY:
                        continue
                    b = 2 * (p % BUFS)
                    wait_free(p, t, first, lagged)
                    if isinstance(turn, tuple):
                        h, c = turn
                        if h % 8 == 0 and c == 0:
                            pe.wait_ge(q_in[h // 8], (t + 1) * 16)
                        if first and h == 0:
                            pe.wait_ge(kst_in[3], 48)
                        score_half(turn, b)
                    if turn == "A" and first:
                        pe.wait_ge(exp_in, 64)
                    if turn == "A" and lagged:
                        replicate(t - 1)
                    if turn == "B" and lagged:
                        attn_out(t - 1)
                    if turn in ("A", "B"):
                        hidden(t, "AB".index(turn))
                    if turn in ("C", "D"):
                        expert_out(t, "CD".index(turn))

            attend(0, True, False)
            with pe.Fori(1, T) as t:
                attend(t, False, True)
            pe.wait_ge(l_slots, T * NC)
            replicate(T - 1)
            attn_out(T - 1)


_INS = ["L0_attn_x", "L0_attn_wq", "L0_attn_wk", "L0_attn_wv", "L0_attn_wo", "L0_attn_q_norm_w", "L0_attn_k_norm_w",
        "L0_ffn_weight", "L0_ffn_ln_gamma", "L0_ffn_ln_beta", "L1_attn_w_in", "L1_attn_b_in", "L1_attn_w_out",
        "L1_attn_b_out", "L1_ffn_Wr", "L1_ffn_br", "L1_ffn_W1", "L1_ffn_b1", "L1_ffn_W2", "L1_ffn_b2"]


def alibi_table():
    import numpy as _np
    slopes = _np.array([(2.0 ** (-8.0 / HEADS)) ** (i + 1) for i in range(HEADS)], dtype=_np.float32)
    own, before = _np.arange(BLK), _np.arange(BLK) - BLK
    tab = _np.zeros((2, BLK, 2, 8, P), _np.float32)
    for b, keys in enumerate((_np.concatenate([own, before]), _np.concatenate([before, own]))):
        rel = keys[None, :] - _np.arange(BLK)[:, None]
        seen = (rel <= 0) & (rel >= -BLK)
        for a in range(2):
            for s in range(8):
                cph, r, cpl = s // 4, s // 2 % 2, s % 2
                tab[a, :, b, s, :] = _np.where(seen, slopes[head_of(cph, r, 2 * cpl + a)] * rel.astype(_np.float32),
                                               BIG)
    return tab.reshape(P, 2, 8, P)


def kernel(**inputs):
    import numpy as _np
    import concourse.bacc as _bacc
    from concourse import mybir as _mybir
    from concourse.bass_utils import run_bass_kernel_spmd as _run

    nc = _bacc.Bacc("TRN2", target_bir_lowering=False, num_devices=1)
    arrays, args = {}, []
    named = [(n, _np.ascontiguousarray(inputs[n])) for n in _INS] + [("alibi", alibi_table())]
    for name, a in named:
        arrays[f"in_{name}"] = a
        args.append(nc.dram_tensor(f"in_{name}", a.shape, _mybir.dt.from_np(a.dtype), kind="ExternalInput").ap())
    shape = inputs["L0_attn_x"].shape
    args.append(nc.dram_tensor("out_0", shape, _mybir.dt.float32, kind="ExternalOutput").ap())
    two_layers(nc, *args)
    r = _run(nc, [arrays], core_ids=[0])
    return r.results[0]["out_0"]
```
